# Optimizing a Trainium2 kernel written in Bass

```python
import numpy as np
import jax
import jax.numpy as jnp

def _softmax(x, axis=-1):
    return jax.nn.softmax(x, axis=axis)

def _gelu(x):
    return jax.nn.gelu(x, approximate=True)

def _silu(x):
    return jax.nn.silu(x)

def _sigmoid(x):
    return jax.nn.sigmoid(x)

def _layernorm(x, axis=-1, eps=1e-05):
    m = jnp.mean(x, axis=axis, keepdims=True)
    v = jnp.var(x, axis=axis, keepdims=True)
    return (x - m) / jnp.sqrt(v + eps)

def _scatter_add(tgt, idx, src, axis=0):
    return tgt.at[idx].add(src)

def _segment_sum(src, seg, n):
    return jax.ops.segment_sum(src, seg, n)
kernel_name = 'mk_adaln_ffn_d2_seqx_r8_e47c89'

def setup_inputs(seed: int=0):
    np.random.seed(seed)
    _w = jnp.asarray

    def _rec_inputs():
        import jax
        import jax.numpy as jnp
        _rk = jax.random.key(seed)
        x = -0.000125 + 0.9999 * jax.random.normal(jax.random.fold_in(_rk, 1), (32, 32, 256), jnp.float32)
        _lenS = 32 - jax.random.randint(jax.random.fold_in(_rk, 7), (32,), 0, max(1, 32 // 4) + 1, jnp.int32)
        _lenS2 = 32 - jax.random.randint(jax.random.fold_in(_rk, 8), (32,), 0, max(1, 32 // 4) + 1, jnp.int32)
        itok_B_0_7 = jax.random.randint(jax.random.fold_in(_rk, 11), (32,), 0, 8, jnp.int32)
        fside_8xS_0 = -0.00162727 + 0.0609077 * jax.random.normal(jax.random.fold_in(_rk, 12), (8, 32), jnp.float32)
        return (x, itok_B_0_7, fside_8xS_0)
    x, itok_B_0_7, fside_8xS_0 = _rec_inputs()

    def _L0_cond_setup():
        import jax, jax.numpy as jnp
        import numpy as np
        B, C, T = (64, 32, 256)
        D, N = (32, 8)
        key = jax.random.key(seed)
        k_x, k_s, k_w, k_b = jax.random.split(key, 4)
        scale = 1.0 / np.sqrt(C)
        x = jax.random.normal(k_x, (B, C, T), dtype=jnp.float32)
        subjects = jax.random.randint(k_s, (B,), 0, N, dtype=jnp.int64)
        weights = jax.random.normal(k_w, (N, C, D), dtype=jnp.float32) * scale
        bias = jax.random.normal(k_b, (N, D), dtype=jnp.float32) * scale
        return {'x': x, 'subjects': subjects, 'weights': weights, 'bias': bias}
    _L0_cond_all = _L0_cond_setup()
    _L0_cond_in = {k: v for k, v in _L0_cond_all.items() if k in ('weights',)}
    del _L0_cond_all

    def _L0_ffn_setup():
        import jax, jax.numpy as jnp
        import numpy as np
        B, S, DIM = (4, 64, 256)
        E, INTER = (32, 128)
        G, TOPK_G, TOPK = (8, 4, 6)
        ROUTE_SCALE = 2.5
        SHARED_INTER = 2 * INTER

        def _gate(xf, gate_w):
            scores = jax.nn.sigmoid(xf @ gate_w.T)
            gs = scores.reshape(-1, G, E // G)
            group_scores = gs.max(axis=-1)
            _, gidx = jax.lax.top_k(group_scores, TOPK_G)
            gmask = jnp.any(jnp.arange(G)[None, None, :] == gidx[:, :, None], axis=1)
            masked = jnp.where(gmask[:, :, None], gs, -jnp.inf).reshape(-1, E)
            _, idx = jax.lax.top_k(masked, TOPK)
            w = jnp.take_along_axis(scores, idx, axis=1)
            w = w / jnp.sum(w, axis=-1, keepdims=True) * ROUTE_SCALE
            return (w, idx)
        key = jax.random.key(seed)
        ks = jax.random.split(key, 8)
        sd = 0.02
        return {'x': jax.random.normal(ks[0], (B, S, DIM), jnp.float32), 'gate_w': jax.random.normal(ks[1], (E, DIM), jnp.float32) * sd, 'w11': jax.random.normal(ks[2], (E, INTER, DIM), jnp.float32) * sd, 'w33': jax.random.normal(ks[3], (E, INTER, DIM), jnp.float32) * sd, 'w22': jax.random.normal(ks[4], (E, DIM, INTER), jnp.float32) * sd, 'sw1': jax.random.normal(ks[5], (SHARED_INTER, DIM), jnp.float32) * sd, 'sw2': jax.random.normal(ks[6], (DIM, SHARED_INTER), jnp.float32) * sd, 'sw3': jax.random.normal(ks[7], (SHARED_INTER, DIM), jnp.float32) * sd}
    _L0_ffn_all = _L0_ffn_setup()
    _L0_ffn_in = {k: v for k, v in _L0_ffn_all.items() if k in ('gate_w', 'w11', 'w33', 'w22', 'sw1', 'sw2', 'sw3')}
    del _L0_ffn_all

    def _L1_cond_setup():
        import jax, jax.numpy as jnp
        import numpy as np
        B, C, D, T, N_SUBJECTS = (128, 32, 32, 256, 8)
        key = jax.random.key(seed)
        kx, ks, kw = jax.random.split(key, 3)
        x = jax.random.normal(kx, (B, C, T), dtype=jnp.float32)
        subjects = jax.random.randint(ks, (B,), 0, N_SUBJECTS, dtype=jnp.int64)
        weights = jax.random.normal(kw, (N_SUBJECTS, C, D), dtype=jnp.float32) * (1.0 / C ** 0.5)
        return {'x': x, 'subjects': subjects, 'weights': weights}
    _L1_cond_all = _L1_cond_setup()
    _L1_cond_in = {k: v for k, v in _L1_cond_all.items() if k in ('weights',)}
    del _L1_cond_all

    def _L1_ffn_setup():
        import jax, jax.numpy as jnp
        import numpy as np

        def fwht(x):
            n = x.shape[-1]
            orig_shape = x.shape
            x = x.reshape(-1, n)
            h = 1
            while h < n:
                x = x.reshape(-1, n // (2 * h), 2, h)
                a = x[:, :, 0, :]
                b = x[:, :, 1, :]
                x = jnp.stack([a + b, a - b], axis=2)
                h *= 2
            x = x.reshape(orig_shape)
            return x * (1.0 / jnp.sqrt(jnp.asarray(n, dtype=x.dtype)))

        def act_quant(x, bits):
            qb = 2.0 ** (bits - 1) - 1.0
            scale = qb / jnp.clip(jnp.max(jnp.abs(x), axis=-1, keepdims=True), 1e-05, None)
            q = jnp.clip(jnp.round(x * scale), -qb, qb) / scale
            return x + jax.lax.stop_gradient(q - x)

        def weight_quant(w):
            scale = jnp.clip(jnp.mean(jnp.abs(w)), 1e-05, None)
            q = jnp.clip(jnp.round(w / scale), -1.0, 1.0) * scale
            return w + jax.lax.stop_gradient(q - w)

        def hbitlinear(x, w, bits):
            xh = fwht(x)
            xq = act_quant(xh, bits)
            wq = weight_quant(w)
            return jnp.einsum('bsh,oh->bso', xq, wq)
        key = jax.random.key(seed)
        k1, k2, k3 = jax.random.split(key, 3)
        B, S, H = (4, 256, 256)
        I = 512
        hidden_states = jax.random.normal(k1, (B, S, H), dtype=jnp.float32)
        w_up = jax.random.normal(k2, (I, H), dtype=jnp.float32) * 0.02
        w_down = jax.random.normal(k3, (H, I), dtype=jnp.float32) * 0.02
        return {'hidden_states': hidden_states, 'w_up': w_up, 'w_down': w_down}
    _L1_ffn_all = _L1_ffn_setup()
    _L1_ffn_in = {k: v for k, v in _L1_ffn_all.items() if k in ('w_up', 'w_down')}
    del _L1_ffn_all
    return {'x': x, 'itok_B_0_7': itok_B_0_7, 'fside_8xS_0': fside_8xS_0, 'L0_cond_weights': _L0_cond_in['weights'], 'L0_ffn_gate_w': _L0_ffn_in['gate_w'], 'L0_ffn_w11': _L0_ffn_in['w11'], 'L0_ffn_w33': _L0_ffn_in['w33'], 'L0_ffn_w22': _L0_ffn_in['w22'], 'L0_ffn_sw1': _L0_ffn_in['sw1'], 'L0_ffn_sw2': _L0_ffn_in['sw2'], 'L0_ffn_sw3': _L0_ffn_in['sw3'], 'L1_cond_weights': _L1_cond_in['weights'], 'L1_ffn_w_up': _L1_ffn_in['w_up'], 'L1_ffn_w_down': _L1_ffn_in['w_down']}

def reference(x, itok_B_0_7, fside_8xS_0, L0_cond_weights, L0_ffn_gate_w, L0_ffn_w11, L0_ffn_w33, L0_ffn_w22, L0_ffn_sw1, L0_ffn_sw2, L0_ffn_sw3, L1_cond_weights, L1_ffn_w_up, L1_ffn_w_down):
    import jax
    import jax.numpy as jnp

    def _L0_cond_ref(x, subjects, weights, bias):
        import jax, jax.numpy as jnp
        import numpy as np
        B, C, T = (64, 32, 256)
        D, N = (32, 8)
        w = weights[subjects]
        b = bias[subjects]
        out = jnp.einsum('bct,bcd->bdt', x, w)
        out = out + b[:, :, None]
        return out

    def _L0_ffn_ref(x, gate_w, w11, w33, w22, sw1, sw2, sw3):
        import jax, jax.numpy as jnp
        import numpy as np
        B, S, DIM = (4, 64, 256)
        E, INTER = (32, 128)
        G, TOPK_G, TOPK = (8, 4, 6)
        ROUTE_SCALE = 2.5
        SHARED_INTER = 2 * INTER

        def _gate(xf, gate_w):
            scores = jax.nn.sigmoid(xf @ gate_w.T)
            gs = scores.reshape(-1, G, E // G)
            group_scores = gs.max(axis=-1)
            _, gidx = jax.lax.top_k(group_scores, TOPK_G)
            gmask = jnp.any(jnp.arange(G)[None, None, :] == gidx[:, :, None], axis=1)
            masked = jnp.where(gmask[:, :, None], gs, -jnp.inf).reshape(-1, E)
            _, idx = jax.lax.top_k(masked, TOPK)
            w = jnp.take_along_axis(scores, idx, axis=1)
            w = w / jnp.sum(w, axis=-1, keepdims=True) * ROUTE_SCALE
            return (w, idx)
        xf = x.reshape(-1, DIM)
        T = xf.shape[0]
        w, idx = _gate(xf, gate_w)
        c = jnp.zeros((T, E), xf.dtype).at[jnp.arange(T)[:, None], idx].add(w)
        g = jnp.einsum('td,eid->tei', xf, w11)
        u = jnp.einsum('td,eid->tei', xf, w33)
        act = jax.nn.silu(g) * u
        y = jnp.einsum('tei,te,edi->td', act, c, w22)
        shared = jax.nn.silu(xf @ sw1.T) * (xf @ sw3.T) @ sw2.T
        return (y + shared).reshape(x.shape)

    def _L1_cond_ref(x, subjects, weights):
        import jax, jax.numpy as jnp
        import numpy as np
        B, C, D, T, N_SUBJECTS = (128, 32, 32, 256, 8)
        w = weights[subjects]
        out = jnp.einsum('bct,bcd->bdt', x, w)
        return out

    def _L1_ffn_ref(hidden_states, w_up, w_down):
        import jax, jax.numpy as jnp
        import numpy as np

        def fwht(x):
            n = x.shape[-1]
            orig_shape = x.shape
            x = x.reshape(-1, n)
            h = 1
            while h < n:
                x = x.reshape(-1, n // (2 * h), 2, h)
                a = x[:, :, 0, :]
                b = x[:, :, 1, :]
                x = jnp.stack([a + b, a - b], axis=2)
                h *= 2
            x = x.reshape(orig_shape)
            return x * (1.0 / jnp.sqrt(jnp.asarray(n, dtype=x.dtype)))

        def act_quant(x, bits):
            qb = 2.0 ** (bits - 1) - 1.0
            scale = qb / jnp.clip(jnp.max(jnp.abs(x), axis=-1, keepdims=True), 1e-05, None)
            q = jnp.clip(jnp.round(x * scale), -qb, qb) / scale
            return x + jax.lax.stop_gradient(q - x)

        def weight_quant(w):
            scale = jnp.clip(jnp.mean(jnp.abs(w)), 1e-05, None)
            q = jnp.clip(jnp.round(w / scale), -1.0, 1.0) * scale
            return w + jax.lax.stop_gradient(q - w)

        def hbitlinear(x, w, bits):
            xh = fwht(x)
            xq = act_quant(xh, bits)
            wq = weight_quant(w)
            return jnp.einsum('bsh,oh->bso', xq, wq)
        ACT_BITS = 8
        h = hbitlinear(hidden_states, w_up, ACT_BITS)
        h = jnp.square(jax.nn.relu(h))
        out = hbitlinear(h, w_down, ACT_BITS)
        return out
    x = x + _L0_ffn_ref(_L0_cond_ref(x, itok_B_0_7, L0_cond_weights, fside_8xS_0), L0_ffn_gate_w, L0_ffn_w11, L0_ffn_w33, L0_ffn_w22, L0_ffn_sw1, L0_ffn_sw2, L0_ffn_sw3)
    x = x + _L1_ffn_ref(_L1_cond_ref(x, itok_B_0_7, L1_cond_weights), L1_ffn_w_up, L1_ffn_w_down)
    return x

_drawn_inputs = setup_inputs


def setup_inputs(seed=0):
    import zlib

    import numpy as np

    out = dict(_drawn_inputs(seed))
    spreads = {}
    factors = {'fside_8xS_0': 8.0,
     'L0_ffn_gate_w': 4.929,
     'L0_ffn_w11': 4.475,
     'L0_ffn_w33': 4.428,
     'L0_ffn_w22': 4.424,
     'L0_ffn_sw1': 3.221,
     'L0_ffn_sw2': 3.19,
     'L0_ffn_sw3': 3.183,
     'L1_cond_weights': 3.678,
     'L1_ffn_w_up': 3.664,
     'L1_ffn_w_down': 3.377}
    for name, (base, spread) in spreads.items():
        noise = np.random.default_rng([zlib.crc32(name.encode()), seed]).standard_normal(out[name].shape)
        drawn = base * np.exp(spread * noise) if base else spread * noise
        out[name] = jnp.asarray(drawn.astype(out[name].dtype))
    for name, factor in factors.items():
        out[name] = (out[name] * factor).astype(out[name].dtype)
    return out
```

```python
from contextlib import ExitStack

import numpy as np

import concourse.bass as bass
from concourse import mybir

P = 128
B, S, D = 32, 32, 256
N = B * S
NT = N // P
NPAIR = NT // 2
BPT = P // S
KD = D // P
SUBJ = 8
E, INTER = 32, 128
GROUPS, TOPK_G, TOPK = 8, 4, 6
ROUTE_SCALE = 2.5
SHARED = 2
EA = E + SHARED
WCOLS = KD * 2 * INTER + D
UP = 512
KU = UP // P
QMAX = 127.0
EPS = 1e-5
MAGIC = 12582912.0

F32 = mybir.dt.float32
BF16 = mybir.dt.bfloat16
I32 = mybir.dt.int32
ALU = mybir.AluOpType
ACT = mybir.ActivationFunctionType
AX = mybir.AxisListType

C_ID, C_HAD, C_IOTA = 0, P, 2 * P
C_DIAG = C_IOTA + SUBJ
C_PART = C_DIAG + BPT
C_END = C_PART + 1


def build(nc, x, subj_rows, subj_cols, bias, gate, experts, cond, w_up, w_down, consts, out):
    ctx = ExitStack()
    with ctx:
        def sb(name, shape, dt=F32):
            return ctx.enter_context(nc.sbuf_tensor(name, shape, dt))

        def sem(name):
            return ctx.enter_context(nc.semaphore(name))

        ps = ctx.enter_context(nc.psum_tensor("ps", [P, 8, 512], F32))

        X = sb("X", [P, NT, D])
        cst = sb("cst", [P, C_END])
        ident = cst[:, C_ID:C_ID + P]
        had = cst[:, C_HAD:C_HAD + P]
        iota = cst[:, C_IOTA:C_IOTA + SUBJ]
        diag = cst[:, C_DIAG:C_DIAG + BPT]
        part = cst[:, C_PART:C_PART + 1]
        identb = sb("identb", [P, P], BF16)
        ones = sb("ones", [P, P])
        magic = sb("magic", [P, 1])
        subj_r = sb("subj_r", [P, NT], I32)
        subj_c = sb("subj_c", [SUBJ, B], I32)
        subj_rf = sb("subj_rf", [P, NT])
        subj_cf = sb("subj_cf", [SUBJ, B])
        mask_r = sb("mask_r", [P, NT, SUBJ])
        mask_c = sb("mask_c", [SUBJ, B])
        bias_s = sb("bias_s", [SUBJ, S])
        bias_m = sb("bias_m", [P, B, S])
        bias_b = sb("bias_b", [P, N])
        cond_w = sb("cond_w", [P, 2, SUBJ, S])
        cond_t = sb("cond_t", [P, NT, SUBJ, S])
        cond_sel = sb("cond_sel", [P, 2, NT, S])
        cond_bd = sb("cond_bd", [P, 2, NT, P])
        gate_s = sb("gate_s", [P, KD, E])
        xfT = sb("xfT", [P, KD, N])
        scores = sb("scores", [P, NT, E])
        gmax = sb("gmax", [P, NT, 2 * GROUPS])
        gtop = sb("gtop", [P, NT, 8])
        grep = sb("grep", [P, NT, 2 * GROUPS])
        gmask = sb("gmask", [P, NT, GROUPS])
        smask = sb("smask", [P, NT, E])
        stop8 = sb("stop8", [P, NT, 8])
        srep = sb("srep", [P, NT, E])
        ssel = sb("ssel", [P, NT, E])
        wsum = sb("wsum", [P, NT])
        wrec = sb("wrec", [P, NT])
        coef = sb("coef", [P, NT, EA])
        W = sb("W", [P, 2, WCOLS])
        sg = sb("sg", [P, 2, 2, INTER])
        h = sb("h", [P, 2, 2, INTER])
        hT = sb("hT", [P, 2, 2 * P])
        up_s = sb("up_s", [P, KD * UP])
        down_s = sb("down_s", [P, KU * D])
        w_abs = sb("w_abs", [P, 2])
        w_tot = sb("w_tot", [P, 2])
        w_inv = sb("w_inv", [P, 2])
        w_t = sb("w_t", [P, 2, KD * UP])
        w_c = sb("w_c", [P, 2, KD * UP], BF16)
        tern = sb("tern", [P, 2, KD * UP], BF16)
        XH = sb("XH", [P, NT, KD, P])
        XHT = sb("XHT", [P, KD, N])
        amax1 = sb("amax1", [P, NT])
        m1 = sb("m1", [P, NT])
        i1 = sb("i1", [P, NT])
        qs1 = sb("qs1", [P, NT])
        f1 = sb("f1", [P, NT])
        fsq = sb("fsq", [P, NT])
        q1t = sb("q1t", [P, NT, D])
        q1c = sb("q1c", [P, NT, D], BF16)
        q1 = sb("q1", [P, NT, D], BF16)
        q1T = sb("q1T", [P, KD, N], BF16)
        r = sb("r", [P, KU, N])
        r2 = sb("r2", [P, KU, N])
        r3 = sb("r3", [P, KU, N])
        amax2 = sb("amax2", [P, NT])
        m2 = sb("m2", [P, NT])
        i2 = sb("i2", [P, NT])
        qs2 = sb("qs2", [P, NT])
        f2 = sb("f2", [P, NT])
        q2t = sb("q2t", [P, 2, UP])
        q2c = sb("q2c", [P, 2, UP], BF16)
        q2 = sb("q2", [P, 2, UP], BF16)
        q2T = sb("q2T", [P, 2, KU, P], BF16)
        Y = sb("Y", [P, NT, D])

        sems = {}

        def named(*names):
            for name in names:
                sems[name] = sem(name)
            return [sems[name] for name in names]

        cst_in, small_in, x_in, gate_in, wq_in, out_done = named("cst_in", "small_in", "x_in", "gate_in", "wq_in", "out_done")
        w_in = named("w_in0", "w_in1")
        filled, bias_ready, cond_ready, bias_psum, bias_b_ready = named("filled", "bias_ready", "cond_ready", "bias_psum", "bias_b_ready")
        xf_psum, xf_ready, logits_psum, scores_ready, coef_ready = named("xf_psum", "xf_ready", "logits_psum", "scores_ready", "coef_ready")
        w_abs_ready, w_tot_psum, w_inv_ready, w_t_ready, tern_ready = named("w_abs_ready", "w_tot_psum", "w_inv_ready", "w_t_ready", "tern_ready")
        gu_ready, sg_ready, h_ready, ht_psum, ht_ready, y_step = named("gu_ready", "sg_ready", "h_ready", "ht_psum", "ht_ready", "y_step")
        x1_ready, xh_ready, sd_psum, xht_ready, hd_psum = named("x1_ready", "xh_ready", "sd_psum", "xht_ready", "hd_psum")
        qs1_ready, q1t_ready, q1_ready, q1T_psum, q1T_ready = named("qs1_ready", "q1t_ready", "q1_ready", "q1T_psum", "q1T_ready")
        up_psum, r_ready, r2_ready, mixed_ready, f_psum = named("up_psum", "r_ready", "r2_ready", "mixed_ready", "f_psum")
        qs2_ready, q2t_ready, q2_ready, q2T_psum, q2T_ready, d_psum, final_ready = named(
            "qs2_ready", "q2t_ready", "q2_ready", "q2T_psum", "q2T_ready", "d_psum", "final_ready")
        dve_chain = sem("dve_chain")

        block = ctx.enter_context(nc.Block())
        STEPS = EA * NPAIR

        @block.sync
        def _(sp):
            sp.dma_start(cst[:, :], consts).then_inc(cst_in, 16)
            sp.dma_start(subj_r[:, :], subj_rows).then_inc(small_in, 16)
            sp.dma_start(subj_c[:, :], subj_cols).then_inc(small_in, 16)
            sp.dma_start(bias_s[:, :], bias).then_inc(small_in, 16)
            sp.dma_start(cond_w[:, :, :, :], cond).then_inc(small_in, 16)
            sp.dma_start(X[:, :, :], x).then_inc(x_in, 16)
            sp.dma_start(gate_s[:, :, :], gate).then_inc(gate_in, 16)
            sp.dma_start(up_s[:, :], w_up).then_inc(wq_in, 16)
            sp.dma_start(down_s[:, :], w_down).then_inc(wq_in, 16)
            for e in range(2):
                sp.dma_start(W[:, e, :], experts[e]).then_inc(w_in[e], 16)
            with sp.Fori(0, EA // 2 - 1) as it:
                for e in range(2):
                    sp.wait_ge(y_step, it * (2 * NPAIR) + (e + 1) * NPAIR)
                    sp.dma_start(W[:, e, :], experts[bass.ds(it * 2 + (e + 2), 1), :, :].rearrange("a p c -> (a p) c")
                                 ).then_inc(w_in[e], 16)
            for i in range(NT):
                sp.wait_ge(final_ready, i + 1)
                sp.dma_start(out[i], Y[:, i, :]).then_inc(out_done, 16)
            sp.wait_ge(out_done, 16 * NT)

        @block.gpsimd
        def _(pool):
            nc.gpsimd.memset(bias_m[:, :, :], 0.0)
            nc.gpsimd.memset(ones[:, :], 1.0)
            nc.gpsimd.memset(magic[:, :], MAGIC)
            nc.gpsimd.memset(gmax[:, :, GROUPS:], -1.0)
            nc.gpsimd.memset(coef[:, :, E:], 1.0)
            pool.wait_ge(cst_in, 16)
            nc.gpsimd.tensor_copy(identb[:, :], ident).then_inc(filled, 1)

        def gu_bank(s):
            return ps[:, 4 + s % 2, :].rearrange("p (t c) -> p t c", t=2)

        @block.tensor
        def _(pe):
            pe.wait_ge(filled, 1)
            pe.wait_ge(bias_ready, 1)
            for n in range(2):
                mm = nc.tensor.matmul(ps[:, 4 + n, :], ones[:, :], bias_m[:, n * 16:(n + 1) * 16, :].rearrange("p b s -> p (b s)"),
                                      start=True, stop=True)
            mm.then_inc(bias_psum, 1)
            pe.wait_ge(x_in, 16)
            pe.wait_ge(cond_ready, 1)
            for i in range(NT):
                for k in range(KD):
                    at = k * 256 + i % 2 * P
                    mm = nc.tensor.matmul(ps[:, i // 2, at:at + P], X[:, i, k * P:(k + 1) * P], cond_bd[:, 0, i, :],
                                          start=True, stop=True)
                if i % 2:
                    mm.then_inc(xf_psum, 1)
            pe.wait_ge(w_abs_ready, 1)
            nc.tensor.matmul(ps[:, 7, 0:2], ones[:, :], w_abs[:, :], start=True, stop=True).then_inc(w_tot_psum, 1)
            pe.wait_ge(gate_in, 16)
            for i in range(NT):
                pe.wait_ge(xf_ready, i // 2 + 1)
                for k in range(KD):
                    mm = nc.tensor.matmul(ps[:, 6, i * E:(i + 1) * E], xfT[:, k, i * P:(i + 1) * P], gate_s[:, k, :],
                                          start=(k == 0), stop=(k == KD - 1))
            mm.then_inc(logits_psum, 1)
            for q in range(NPAIR):
                nc.tensor.matmul(ps[:, q, :], ident, X[:, 2 * q:2 * q + 2, :].rearrange("p t c -> p (t c)"),
                                 start=True, stop=False, skip_group_check=True)

            def gate_up(s, e):
                q = s % NPAIR
                for t in range(2):
                    i = 2 * q + t
                    for k in range(KD):
                        mm = nc.tensor.matmul(gu_bank(s)[:, t, :], xfT[:, k, i * P:(i + 1) * P],
                                              W[:, e, k * 256:(k + 1) * 256], start=(k == 0), stop=(k == KD - 1))
                mm.then_inc(gu_ready, 1)

            def turn(s):
                for t in range(2):
                    mm = nc.tensor.transpose(ps[:, 6 + s % 2, t * P:(t + 1) * P], h[:, s % 2, t, :], ident)
                mm.then_inc(ht_psum, 1)

            def down(s, e):
                q = s % NPAIR
                for t in range(2):
                    mm = nc.tensor.matmul(ps[:, q, t * D:(t + 1) * D], hT[:, s % 2, t * P:(t + 1) * P],
                                          W[:, e, 512:512 + D], start=False, stop=False, skip_group_check=True)
                mm.then_inc(y_step, 1)

            def steps(s0, last):
                for j in range(2 * NPAIR):
                    if not last or j + 2 < 2 * NPAIR:
                        if (j + 2) % NPAIR == 0:
                            e = (j + 2) // NPAIR
                            pe.wait_ge(w_in[e % 2], s0 * (16 // (2 * NPAIR)) + 16 * (e // 2 + 1))
                        pe.wait_ge(h_ready, s0 + (j + 1))
                        gate_up(j + 2, (j + 2) // NPAIR % 2)
                    if not last or j + 1 < 2 * NPAIR:
                        pe.wait_ge(h_ready, s0 + (j + 2))
                        turn(j + 1)
                    pe.wait_ge(ht_ready, s0 + (j + 1))
                    down(j, j // NPAIR)

            pe.wait_ge(bias_b_ready, 1)
            pe.wait_ge(scores_ready, 1)
            pe.wait_ge(w_inv_ready, 1)
            pe.wait_ge(w_in[0], 16)
            gate_up(0, 0)
            gate_up(1, 0)
            pe.wait_ge(h_ready, 1)
            turn(0)
            with pe.Fori(0, EA // 2 - 1) as it:
                steps(it * (2 * NPAIR), False)
            steps(STEPS - 2 * NPAIR, True)

            def halves(q):
                pe.wait_ge(xh_ready, q + 1)
                if q >= 2:
                    pe.wait_ge(xht_ready, q - 1)
                for t in range(2):
                    for a in range(KD):
                        at = a * 256 + t * P
                        mm = nc.tensor.matmul(ps[:, 4 + q % 2, at:at + P], XH[:, 2 * q + t, a, :], cond_bd[:, 1, 2 * q + t, :],
                                              start=True, stop=True)
                mm.then_inc(sd_psum, 1)

            def hadamard1(q):
                pe.wait_ge(xht_ready, q + 1)
                if q >= 2:
                    pe.wait_ge(q1t_ready, q - 1)
                for t in range(2):
                    i = 2 * q + t
                    for a in range(KD):
                        at = t * 256 + a * P
                        mm = nc.tensor.matmul(ps[:, 6 + q % 2, at:at + P], XHT[:, a, i * P:(i + 1) * P], had,
                                              start=True, stop=True)
                mm.then_inc(hd_psum, 1)

            def turn1(q):
                pe.wait_ge(q1_ready, q + 1)
                if q >= 2:
                    pe.wait_ge(q1T_ready, q - 1)
                bank = ps[:, q % 2, :].bitcast(BF16)
                for t in range(2):
                    for k in range(KD):
                        at = k * 256 + t * P
                        mm = nc.tensor.transpose(bank[:, at:at + P], q1[:, 2 * q + t, k * P:(k + 1) * P], identb[:, :])
                mm.then_inc(q1T_psum, 1)

            def up(half):
                pe.wait_ge(q1T_ready, 2 * half + 2)
                for m in range(KU):
                    u = KU * half + m
                    if u >= 2:
                        pe.wait_ge(r2_ready, u - 1)
                    for k in range(KD):
                        mm = nc.tensor.matmul(ps[:, 2 + u % 2, :], tern[:, 0, k * UP + m * P:k * UP + (m + 1) * P],
                                              q1T[:, k, half * 512:(half + 1) * 512], start=(k == 0), stop=(k == KD - 1))
                    mm.then_inc(up_psum, 1)

            pe.wait_ge(cond_ready, 2)
            pe.wait_ge(x1_ready, NPAIR)
            for q in range(NPAIR + 2):
                if q < NPAIR:
                    halves(q)
                if 1 <= q <= NPAIR:
                    hadamard1(q - 1)
                if q >= 2:
                    turn1(q - 2)
            pe.wait_ge(tern_ready, 1)
            up(0)
            up(1)

            def hadamard2(i):
                pe.wait_ge(mixed_ready, i // 4 + 1)
                if i >= 4:
                    pe.wait_ge(q2t_ready, i - 3)
                for a in range(KU):
                    mm = nc.tensor.matmul(ps[:, 4 + i % 4, a * P:(a + 1) * P], r2[:, a, i * P:(i + 1) * P], had,
                                          start=True, stop=True)
                mm.then_inc(f_psum, 1)

            def turn2(i):
                pe.wait_ge(q2_ready, i + 1)
                if i >= 2:
                    pe.wait_ge(q2T_ready, i - 1)
                bank = ps[:, i % 2, :].bitcast(BF16)
                for a in range(KU):
                    mm = nc.tensor.transpose(bank[:, a * P:(a + 1) * P], q2[:, i % 2, a * P:(a + 1) * P], identb[:, :])
                mm.then_inc(q2T_psum, 1)

            def down2(i):
                pe.wait_ge(q2T_ready, i + 1)
                if i >= 2:
                    pe.wait_ge(final_ready, i - 1)
                for a in range(KU):
                    mm = nc.tensor.matmul(ps[:, 2 + i % 2, 0:D], q2T[:, i % 2, a, :], tern[:, 1, a * D:(a + 1) * D],
                                          start=(a == 0), stop=(a == KU - 1))
                mm.then_inc(d_psum, 1)

            for i in range(NT + 2):
                if i < NT:
                    hadamard2(i)
                if 1 <= i <= NT:
                    turn2(i - 1)
                if i >= 2:
                    down2(i - 2)

        @block.scalar
        def _(act):
            act.wait_ge(bias_psum, 1)
            nc.scalar.copy(bias_b[:, :], ps[:, 4:6, :].rearrange("p n c -> p (n c)")).then_inc(bias_b_ready, 1)
            act.wait_ge(w_inv_ready, 1)
            for n, w in enumerate((up_s, down_s)):
                ins = nc.scalar.activation(w_t[:, n, :], w[:, :], ACT.Identity, bias=magic[:, :], scale=w_inv[:, n:n + 1])
            ins.then_inc(w_t_ready, 1)
            act.wait_ge(logits_psum, 1)
            nc.scalar.activation(scores[:, :, :].rearrange("p i e -> p (i e)"), ps[:, 6, 0:NT * E], ACT.Sigmoid).then_inc(scores_ready, 1)

            def silu(s):
                nc.scalar.activation(sg[:, s % 2, :, :], gu_bank(s)[:, :, 0:INTER], ACT.Silu).then_inc(sg_ready, 1)

            def copy(s):
                nc.scalar.copy(hT[:, s % 2, :], ps[:, 6 + s % 2, 0:256]).then_inc(ht_ready, 1)

            def steps(s0, last):
                for j in range(2 * NPAIR):
                    if not last or j + 1 < 2 * NPAIR:
                        act.wait_ge(gu_ready, s0 + (j + 2))
                        silu(j + 1)
                    act.wait_ge(ht_psum, s0 + (j + 1))
                    copy(j)

            act.wait_ge(gu_ready, 1)
            silu(0)
            with act.Fori(0, EA // 2 - 1) as it:
                steps(it * (2 * NPAIR), False)
            steps(STEPS - 2 * NPAIR, True)

            act.wait_ge(y_step, STEPS)
            for q in range(NPAIR):
                nc.scalar.copy(X[:, 2 * q:2 * q + 2, :].rearrange("p t c -> p (t c)"), ps[:, q, :]).then_inc(x1_ready, 1)

            def xht(q):
                act.wait_ge(sd_psum, q + 1)
                nc.scalar.copy(XHT[:, :, q * 256:(q + 1) * 256], ps[:, 4 + q % 2, :].rearrange("p (a n) -> p a n", a=KD)
                               ).then_inc(xht_ready, 1)

            def q1t_(q):
                act.wait_ge(qs1_ready, q + 1)
                for t in range(2):
                    ins = nc.scalar.activation(q1t[:, 2 * q + t, :], ps[:, 6 + q % 2, t * 256:(t + 1) * 256], ACT.Identity,
                                               bias=magic[:, :], scale=qs1[:, 2 * q + t:2 * q + t + 1])
                ins.then_inc(q1t_ready, 1)

            def q1T_(q):
                act.wait_ge(q1T_psum, q + 1)
                nc.scalar.copy(q1T[:, :, q * 256:(q + 1) * 256],
                               ps[:, q % 2, :].bitcast(BF16)[:, 0:512].rearrange("p (k n) -> p k n", k=KD)).then_inc(q1T_ready, 1)

            def relu(u):
                act.wait_ge(up_psum, u + 1)
                half, m = divmod(u, KU)
                nc.scalar.activation(r[:, m, half * 512:(half + 1) * 512], ps[:, 2 + u % 2, :], ACT.Relu).then_inc(r_ready, 1)

            for q in range(NPAIR + 2):
                if q < NPAIR:
                    xht(q)
                if 1 <= q <= NPAIR:
                    q1t_(q - 1)
                if q >= 2:
                    q1T_(q - 2)
            for u in range(2 * KU):
                relu(u)
            for i in range(NT + 1):
                if i < NT:
                    act.wait_ge(qs2_ready, i + 1)
                    if i >= 2:
                        act.wait_ge(q2_ready, i - 1)
                    nc.scalar.activation(q2t[:, i % 2, :], ps[:, 4 + i % 4, :], ACT.Identity, bias=magic[:, :],
                                         scale=qs2[:, i:i + 1]).then_inc(q2t_ready, 1)
                if i >= 1:
                    act.wait_ge(q2T_psum, i)
                    if i >= 3:
                        act.wait_ge(d_psum, i - 2)
                    nc.scalar.copy(q2T[:, (i - 1) % 2, :, :].rearrange("p a n -> p (a n)"),
                                   ps[:, (i - 1) % 2, :].bitcast(BF16)[:, 0:512]).then_inc(q2T_ready, 1)

        @block.vector
        def _(v):
            chained = [0]

            def link(ins):
                chained[0] += 1
                ins.then_inc(dve_chain, 1)
                v.wait_ge(dve_chain, chained[0])

            V = nc.vector

            def bc(ap, dims, shape):
                for d in dims:
                    ap = ap.unsqueeze(d)
                return ap.broadcast_to(shape)

            v.wait_ge(cst_in, 16)
            v.wait_ge(small_in, 64)
            V.tensor_copy(subj_rf[:, :], subj_r[:, :])
            link(V.tensor_copy(subj_cf[:, :], subj_c[:, :]))
            link(V.tensor_scalar(mask_c[:, :], subj_cf[:, :], part[0:SUBJ, :], None, ALU.is_equal))
            v.wait_ge(filled, 1)
            V.tensor_tensor(bias_m[0:SUBJ, :, :], bc(bias_s[:, :], [1], [SUBJ, B, S]), bc(mask_c[:, :], [2], [SUBJ, B, S]),
                            ALU.mult).then_inc(bias_ready, 1)
            link(V.tensor_tensor(mask_r[:, :, :], bc(subj_rf[:, :], [2], [P, NT, SUBJ]), bc(iota, [1], [P, NT, SUBJ]),
                                 ALU.is_equal))

            def condition(layer):
                link(V.tensor_tensor(cond_t[:, :, :, :], bc(cond_w[:, layer, :, :], [1], [P, NT, SUBJ, S]),
                                     bc(mask_r[:, :, :], [3], [P, NT, SUBJ, S]), ALU.mult))
                link(V.tensor_reduce(cond_sel[:, layer, :, :], cond_t[:, :, :, :].rearrange("p i n s -> p i s n"), AX.X, ALU.add))
                V.tensor_tensor(cond_bd[:, layer, :, :].rearrange("p i (j s) -> p i j s", j=BPT),
                                bc(cond_sel[:, layer, :, :], [2], [P, NT, BPT, S]),
                                bc(bc(diag, [1], [P, NT, BPT]), [3], [P, NT, BPT, S]), ALU.mult).then_inc(cond_ready, 1)

            condition(0)
            v.wait_ge(wq_in, 32)
            V.tensor_reduce(w_abs[:, 0:1], up_s[:, :], AX.X, ALU.add, apply_absolute_value=True)
            V.tensor_reduce(w_abs[:, 1:2], down_s[:, :], AX.X, ALU.add, apply_absolute_value=True).then_inc(w_abs_ready, 1)
            v.wait_ge(bias_b_ready, 1)
            for q in range(NPAIR):
                v.wait_ge(xf_psum, q + 1)
                V.tensor_tensor(xfT[:, :, q * 256:(q + 1) * 256], ps[:, q, :].rearrange("p (k n) -> p k n", k=KD),
                                bc(bias_b[:, q * 256:(q + 1) * 256], [1], [P, KD, 256]), ALU.add).then_inc(xf_ready, 1)
            v.wait_ge(w_tot_psum, 1)
            link(V.tensor_scalar(w_tot[:, :], ps[:, 7, 0:2], 1.0 / (UP * D), EPS, ALU.mult, ALU.max))
            V.reciprocal(w_inv[:, :], w_tot[:, :]).then_inc(w_inv_ready, 1)
            v.wait_ge(w_t_ready, 1)
            link(V.tensor_scalar(w_c[:, :, :], w_t[:, :, :], MAGIC, 1.0, ALU.subtract, ALU.min))
            V.tensor_scalar(tern[:, :, :], w_c[:, :, :], -1.0, None, ALU.max).then_inc(tern_ready, 1)

            v.wait_ge(scores_ready, 1)
            link(V.tensor_reduce(gmax[:, :, 0:GROUPS], scores[:, :, :].rearrange("p i (g m) -> p i g m", g=GROUPS), AX.X, ALU.max))
            for i in range(NT):
                ins = V.max(gtop[:, i, :], gmax[:, i, 0:GROUPS])
            link(ins)
            link(V.memset(gtop[:, :, TOPK_G:], -1.0))
            for i in range(NT):
                ins = V.match_replace(grep[:, i, :], gtop[:, i, :], gmax[:, i, :], -2.0)
            link(ins)
            link(V.tensor_scalar(gmask[:, :, :], grep[:, :, 0:GROUPS], 0.0, None, ALU.is_lt))
            four = [P, NT, GROUPS, E // GROUPS]
            link(V.tensor_tensor(smask[:, :, :].rearrange("p i (g m) -> p i g m", g=GROUPS),
                                 scores[:, :, :].rearrange("p i (g m) -> p i g m", g=GROUPS),
                                 bc(gmask[:, :, :], [3], four), ALU.mult))
            link(V.tensor_scalar(gmask[:, :, :], gmask[:, :, :], 1.0, None, ALU.subtract))
            link(V.tensor_tensor(smask[:, :, :].rearrange("p i (g m) -> p i g m", g=GROUPS),
                                 smask[:, :, :].rearrange("p i (g m) -> p i g m", g=GROUPS),
                                 bc(gmask[:, :, :], [3], four), ALU.add))
            for i in range(NT):
                ins = V.max(stop8[:, i, :], smask[:, i, :])
            link(ins)
            link(V.memset(stop8[:, :, TOPK:], -1.0))
            for i in range(NT):
                ins = V.match_replace(srep[:, i, :], stop8[:, i, :], smask[:, i, :], -2.0)
            link(ins)
            link(V.tensor_scalar(smask[:, :, :], smask[:, :, :], 0.0, None, ALU.is_ge))
            link(V.scalar_tensor_tensor(ssel[:, :, :], srep[:, :, :], 0.0, smask[:, :, :], ALU.is_lt, ALU.mult))
            link(V.tensor_tensor(scores[:, :, :], scores[:, :, :], ssel[:, :, :], ALU.mult))
            link(V.tensor_reduce(wsum[:, :], scores[:, :, :], AX.X, ALU.add))
            link(V.reciprocal(wrec[:, :], wsum[:, :]))
            link(V.scalar_tensor_tensor(coef[:, :, 0:E], scores[:, :, :], ROUTE_SCALE, bc(wrec[:, :], [2], [P, NT, E]),
                                        ALU.mult, ALU.mult))

            def steps(s0, e0):
                for j in range(2 * NPAIR):
                    v.wait_ge(sg_ready, s0 + (j + 1))
                    for t in range(2):
                        i = 2 * (j % NPAIR) + t
                        ins = V.scalar_tensor_tensor(h[:, j % 2, t, :], sg[:, j % 2, t, :],
                                                     coef[:, i, bass.ds(e0 + j // NPAIR, 1)],
                                                     gu_bank(j)[:, t, INTER:], ALU.mult, ALU.mult)
                    ins.then_inc(h_ready, 1)

            with v.Fori(0, EA // 2) as it:
                steps(it * (2 * NPAIR), it * 2)

            condition(1)
            for q in range(NPAIR):
                v.wait_ge(x1_ready, q + 1)
                two = X[:, 2 * q:2 * q + 2, :]
                V.tensor_tensor(XH[:, 2 * q:2 * q + 2, 0, :], two[:, :, 0:P], two[:, :, P:D], ALU.add)
                V.tensor_tensor(XH[:, 2 * q:2 * q + 2, 1, :], two[:, :, 0:P], two[:, :, P:D], ALU.subtract).then_inc(xh_ready, 1)

            def stats1(q):
                v.wait_ge(hd_psum, q + 1)
                at = slice(2 * q, 2 * q + 2)
                link(V.tensor_reduce(amax1[:, at], ps[:, 6 + q % 2, :].rearrange("p (t c) -> p t c", t=2), AX.X, ALU.max,
                                     apply_absolute_value=True))
                link(V.tensor_scalar(m1[:, at], amax1[:, at], float(D) ** -0.5, EPS, ALU.mult, ALU.max))
                link(V.reciprocal(i1[:, at], m1[:, at]))
                V.tensor_scalar(qs1[:, at], i1[:, at], QMAX * float(D) ** -0.5, None, ALU.mult).then_inc(qs1_ready, 1)

            def clip1(q):
                v.wait_ge(q1t_ready, q + 1)
                at = slice(2 * q, 2 * q + 2)
                link(V.tensor_scalar(q1c[:, at, :], q1t[:, at, :], MAGIC, QMAX, ALU.subtract, ALU.min))
                V.tensor_scalar(q1[:, at, :], q1c[:, at, :], -QMAX, None, ALU.max).then_inc(q1_ready, 1)

            for q in range(NPAIR + 1):
                if q < NPAIR:
                    stats1(q)
                if q >= 1:
                    clip1(q - 1)
            link(V.tensor_scalar(f1[:, :], m1[:, :], w_tot[:, 0:1], 1.0 / QMAX, ALU.mult, ALU.mult))
            link(V.tensor_tensor(fsq[:, :], f1[:, :], f1[:, :], ALU.mult))
            link(V.tensor_scalar(fsq[:, :], fsq[:, :], float(UP) ** -0.5, None, ALU.mult))

            def square(u):
                half, m = divmod(u, KU)
                at = slice(half * 512, (half + 1) * 512)
                v.wait_ge(r_ready, u + 1)
                V.tensor_tensor(r2[:, m, at], r[:, m, at], ps[:, 2 + u % 2, :], ALU.mult).then_inc(r2_ready, 1)

            def mix(half):
                at = slice(half * 512, (half + 1) * 512)
                a = r2[:, :, at].rearrange("p (c d) n -> p c d n", c=2)
                b = r3[:, :, at].rearrange("p (c d) n -> p c d n", c=2)
                v.wait_ge(r2_ready, KU * (half + 1))
                V.tensor_tensor(b[:, :, 0, :], a[:, :, 0, :], a[:, :, 1, :], ALU.add)
                link(V.tensor_tensor(b[:, :, 1, :], a[:, :, 0, :], a[:, :, 1, :], ALU.subtract))
                V.tensor_tensor(a[:, 0, :, :], b[:, 0, :, :], b[:, 1, :, :], ALU.add)
                V.tensor_tensor(a[:, 1, :, :], b[:, 0, :, :], b[:, 1, :, :], ALU.subtract).then_inc(mixed_ready, 1)

            for half in range(2):
                for u in range(KU):
                    square(KU * half + u)
                mix(half)

            def stats2(i):
                v.wait_ge(f_psum, i + 1)
                at = slice(i, i + 1)
                link(V.tensor_reduce(amax2[:, at], ps[:, 4 + i % 4, :], AX.X, ALU.max, apply_absolute_value=True))
                link(V.tensor_scalar(m2[:, at], amax2[:, at], fsq[:, at], EPS, ALU.mult, ALU.max))
                link(V.reciprocal(i2[:, at], m2[:, at]))
                V.tensor_scalar(qs2[:, at], i2[:, at], fsq[:, at], QMAX, ALU.mult, ALU.mult).then_inc(qs2_ready, 1)
                link(V.tensor_scalar(f2[:, at], m2[:, at], w_tot[:, 1:2], 1.0 / QMAX, ALU.mult, ALU.mult))

            def clip2(i):
                v.wait_ge(q2t_ready, i + 1)
                if i >= 2:
                    v.wait_ge(q2T_psum, i - 1)
                link(V.tensor_scalar(q2c[:, i % 2, :], q2t[:, i % 2, :], MAGIC, QMAX, ALU.subtract, ALU.min))
                V.tensor_scalar(q2[:, i % 2, :], q2c[:, i % 2, :], -QMAX, None, ALU.max).then_inc(q2_ready, 1)

            def final(i):
                v.wait_ge(d_psum, i + 1)
                V.scalar_tensor_tensor(Y[:, i, :], ps[:, 2 + i % 2, 0:D], f2[:, i:i + 1], X[:, i, :],
                                       ALU.mult, ALU.add).then_inc(final_ready, 1)

            for i in range(NT + 2):
                if i < NT:
                    stats2(i)
                if 1 <= i <= NT:
                    clip2(i - 1)
                if i >= 2:
                    final(i - 2)


def hadamard(n):
    m = np.ones((1, 1), np.float32)
    while m.shape[0] < n:
        m = np.block([[m, m], [m, -m]])
    return m


def constants():
    c = np.zeros((P, C_END), np.float32)
    c[:, C_ID:C_ID + P] = np.eye(P)
    c[:, C_HAD:C_HAD + P] = hadamard(P)
    c[:, C_IOTA:C_IOTA + SUBJ] = np.arange(SUBJ)
    c[:, C_DIAG:C_DIAG + BPT] = np.arange(P)[:, None] // S == np.arange(BPT)
    c[:, C_PART] = np.arange(P)
    return c


def kernel(**inputs):
    import concourse.bacc as _bacc
    from concourse.bass_utils import run_bass_kernel_spmd as _run

    a = {k: np.asarray(v) for k, v in inputs.items()}
    subj = a["itok_B_0_7"]
    x = a["x"].reshape(NT, P, D).transpose(1, 0, 2)

    def cond(w):
        return np.tile(w.transpose(1, 0, 2), (BPT, 1, 1))

    def inward(w):
        t = np.swapaxes(w, -1, -2)
        t = t.reshape(*t.shape[:-2], KD, P, t.shape[-1])
        return np.swapaxes(t, -3, -2)

    def expert(w1, w3, w2):
        gu = np.concatenate([inward(w1), inward(w3)], -1).reshape(-1, P, KD * 2 * INTER)
        return np.concatenate([gu, np.swapaxes(w2, -1, -2)], -1)

    sw = [a["L0_ffn_sw1"].reshape(SHARED, INTER, D), a["L0_ffn_sw3"].reshape(SHARED, INTER, D),
          a["L0_ffn_sw2"].reshape(D, SHARED, INTER).transpose(1, 0, 2)]
    arrays = {
        "x": x,
        "subj_rows": np.repeat(subj.reshape(NT, BPT).T, S, axis=0),
        "subj_cols": np.broadcast_to(subj, (SUBJ, B)),
        "bias": a["fside_8xS_0"],
        "gate": inward(a["L0_ffn_gate_w"]),
        "experts": np.concatenate([expert(a["L0_ffn_w11"], a["L0_ffn_w33"], a["L0_ffn_w22"]), expert(*sw)]),
        "cond": np.stack([cond(a["L0_cond_weights"]), cond(a["L1_cond_weights"])], 1),
        "w_up": inward(a["L1_ffn_w_up"]).reshape(P, KD * UP),
        "w_down": a["L1_ffn_w_down"].T.reshape(KU, P, D).transpose(1, 0, 2).reshape(P, KU * D),
        "consts": constants(),
    }
    arrays = {k: np.ascontiguousarray(v) for k, v in arrays.items()}
    nc = _bacc.Bacc("TRN2", target_bir_lowering=False, num_devices=1)
    aps = {k: nc.dram_tensor(f"in_{k}", v.shape, mybir.dt.from_np(v.dtype), kind="ExternalInput").ap() for k, v in arrays.items()}
    out = nc.dram_tensor("out_0", (NT, P, D), F32, kind="ExternalOutput").ap()
    build(nc, out=out, **aps)
    res = _run(nc, [{f"in_{k}": v for k, v in arrays.items()}], core_ids=[0])
    return res.results[0]["out_0"].reshape(B, S, D)
```

```python
from contextlib import ExitStack

import numpy as np

import concourse.bass as bass
from concourse import mybir

P = 128
B, S, D = 32, 32, 256
N = B * S
NT = N // P
NPAIR = NT // 2
BPT = P // S
KD = D // P
SUBJ = 8
E, INTER = 32, 128
GROUPS, TOPK_G, TOPK = 8, 4, 6
ROUTE_SCALE = 2.5
SHARED = 2
EA = E + SHARED
WCOLS = KD * 2 * INTER + D
TILES = -(-(N * TOPK // P + E - 1) // 8) * 8
UNROLL = 4
STEPS = TILES // 2
ROUNDS = STEPS // UNROLL
HOT = 4
UP = 512
KU = UP // P
QMAX = 127.0
TAIL = [(i, 2) for i in range(0, NT - 2, 2)] + [(NT - 2, 1), (NT - 1, 1)]
EPS = 1e-5
MAGIC = 12582912.0

F32 = mybir.dt.float32
F16 = mybir.dt.float16
BF16 = mybir.dt.bfloat16
I32 = mybir.dt.int32
ALU = mybir.AluOpType
ACT = mybir.ActivationFunctionType
AX = mybir.AxisListType

C_ID = 0
C_HAD = C_ID + P
C_LOWER = C_HAD + 3 * P
C_IOTA = C_LOWER + P
C_DIAG = C_IOTA + P
C_TOKEN = C_DIAG + BPT
C_END = C_TOKEN + NT


def build(nc, x, subj_rows, bias, gate, experts, cond, w_up, w_down, consts, out, xf_dram, y_dram):
    ctx = ExitStack()
    with ctx:
        def sb(name, shape, dt=F32):
            return ctx.enter_context(nc.sbuf_tensor(name, shape, dt))

        def sem(name):
            return ctx.enter_context(nc.semaphore(name))

        ps = ctx.enter_context(nc.psum_tensor("ps", [P, 8, 512], F32))

        X = sb("X", [P, NT, D])
        cst = sb("cst", [P, C_END])
        ident, had, lower = (cst[:, c:c + P] for c in (C_ID, C_HAD, C_LOWER))
        had_rows = [cst[:, C_HAD + a * P:C_HAD + (a + 2) * P] for a in range(KD)]
        iota = cst[:, C_IOTA:C_IOTA + P]
        diag = cst[:, C_DIAG:C_DIAG + BPT]
        token = cst[:, C_TOKEN:C_TOKEN + NT]
        identb = sb("identb", [P, P], BF16)
        lowerb = sb("lowerb", [P, P], BF16)
        onesb = sb("onesb", [P, P], BF16)
        ones = sb("ones", [P, P])
        iota16 = sb("iota16", [P, P], F16)
        magic = sb("magic", [P, 1])
        subj = sb("subj", [P, NT], I32)
        subj_f = sb("subj_f", [P, NT])
        subj_mask = sb("subj_mask", [P, NT, SUBJ])
        bias_s = sb("bias_s", [P, SUBJ])
        bias_t = sb("bias_t", [P, NT, SUBJ])
        bias_row = sb("bias_row", [P, NT])
        cond_w = sb("cond_w", [P, 2, SUBJ, S])
        cond_sel = sb("cond_sel", [P, 2, NT, S])
        cond_bd = sb("cond_bd", [P, 2, NT, P])
        gate_s = sb("gate_s", [P, KD, E])
        rows_area = sb("rows_area", [P, NT * D])
        rows = rows_area[:, :].rearrange("p (i d) -> p i d", i=NT)
        xcT = rows_area[:, :].rearrange("p (a n) -> p a n", a=KD)
        xT_area = sb("xT_area", [P, NT * D])
        xT = xT_area[:, :].rearrange("p (k n) -> p k n", k=KD)
        scores = sb("scores", [P, NT, E])
        gmax = sb("gmax", [P, NT, 2 * GROUPS])
        gtop = sb("gtop", [P, NT, 8])
        grep = sb("grep", [P, NT, 2 * GROUPS])
        gmask = sb("gmask", [P, NT, GROUPS])
        smask = sb("smask", [P, NT, E])
        stop8 = sb("stop8", [P, NT, 8])
        srep = sb("srep", [P, NT, E])
        chosen = sb("chosen", [P, NT, E], BF16)
        wsum = sb("wsum", [P, NT])
        wrec = sb("wrec", [P, NT])
        tiles_of = sb("tiles_of", [P, E])
        tiles_end = sb("tiles_end", [P, E])
        tiles_from = sb("tiles_from", [P, E])
        begun = sb("begun", [P, E])
        tile_e = sb("tile_e", [P, 1])
        expert_of = sb("expert_of", [1, TILES], I32)
        turnover = srep
        place = sb("place", [P, NT, E])
        place8 = sb("place8", [P, NT, 8])
        part8 = sb("part8", [P, NT, 8])
        tile8 = sb("tile8", [P, NT, 8])
        fetch = sb("fetch", [P, NT, 8], I32)
        weight = sb("weight", [P, NT, TOPK])
        slot_token = sb("slot_token", [P, TILES], I32)
        now = sb("now", [P, UNROLL, 2], I32)
        W = sb("W", [P, EA, WCOLS])
        wflat = W[:, :, :].rearrange("p e c -> p (e c)")
        YG, NR = NT * TOPK * D, KU * 2 * P
        yg = wflat[:, 0:YG].rearrange("p (i k d) -> p i k d", i=NT, k=TOPK)
        r, r2, r3, r4 = (wflat[:, YG + n * NR:YG + (n + 1) * NR].rearrange("p (m n) -> p m n", m=KU) for n in range(4))
        sg = sb("sg", [P, 2, 2, INTER])
        h = sb("h", [P, 2, 2, INTER])
        hT = sb("hT", [P, 2, 2 * P])
        xg_area = sb("xg_area", [P, UNROLL * 2 * D])
        xg = xg_area[:, :].rearrange("p (u t d) -> p u t d", u=UNROLL, t=2)
        q1c, q1 = (xg_area[:, n * 1024:(n + 1) * 1024].bitcast(BF16).rearrange("p (i d) -> p i d", i=NT) for n in range(2))
        xgT_area = sb("xgT_area", [P, 2 * 512])
        xgT = xgT_area[:, :].rearrange("p (u t k n) -> p u t k n", u=2, t=2, k=KD)
        q1T = xgT_area[:, :].bitcast(BF16).rearrange("p (k n) -> p k n", k=KD)
        y_area = sb("y_area", [P, UNROLL * 2 * D])
        yv = y_area[:, :].rearrange("p (u c) -> p u c", u=UNROLL)
        match = y_area[:, 0:NT * TOPK * E].rearrange("p (i k e) -> p i k e", i=NT, k=TOPK)
        hot_row = y_area[:, 0:HOT * TOPK * P // 2].bitcast(F16).rearrange("p (r k c) -> p r k c", r=HOT, k=TOPK)
        hot_tile = xg_area[:, 0:HOT * TOPK * TILES // 2].bitcast(F16).rearrange("p (r k c) -> p r k c", r=HOT, k=TOPK)
        wq_area = sb("wq_area", [P, 2048])
        up_s, down_s = wq_area[:, 0:1024], wq_area[:, 1024:2048]
        q1t = wq_area[:, :].rearrange("p (i d) -> p i d", i=NT)
        w_abs = sb("w_abs", [P, 2])
        w_tot = sb("w_tot", [P, 2])
        w_inv = sb("w_inv", [P, 2])
        w_up_scaled = sb("w_up_scaled", [P, 1])
        wt_area = sb("wt_area", [P, 2048])
        w_t = wt_area[:, :].rearrange("p (n c) -> p n c", n=2)
        q2c, q2, q2T = (wt_area[:, n * 512:(n + 1) * 512].bitcast(BF16).rearrange("p (t c) -> p t c", t=2) for n in range(3))
        wc_area = sb("wc_area", [P, 1024])
        w_c = wc_area[:, :].bitcast(BF16).rearrange("p (n c) -> p n c", n=2)
        q2t = wc_area[:, :].rearrange("p (t c) -> p t c", t=2)
        tern = sb("tern", [P, 2, KD * UP], BF16)
        amax1, m1, qs1, f1, fsq, guard2, amax2, m2, qs2, f2 = (
            sb(n, [P, NT]) for n in "amax1 m1 qs1 f1 fsq guard2 amax2 m2 qs2 f2".split())

        def named(names):
            return [sem(name) for name in names.split()]

        cst_in, small_in, x_in, gate_in, wq_in, sw_in, w_in, xf_out, out_done = named(
            "cst_in small_in x_in gate_in wq_in sw_in w_in xf_out out_done")
        xg_in = named(" ".join(f"xg_in{u}" for u in range(UNROLL)))
        y_out = named(" ".join(f"y_out{u}" for u in range(UNROLL)))
        yg_in = [named(" ".join(f"yg_in{g}_{k}" for k in range(TOPK))) for g in range(len(TAIL))]
        filled, cond_ready, rows_psum, rows_ready, xT_psum, xT_ready, logits_psum, scores_ready = named(
            "filled cond_ready rows_psum rows_ready xT_psum xT_ready logits_psum scores_ready")
        w_abs_ready, w_tot_psum, w_inv_ready, w_t_ready, tern_ready = named("w_abs_ready w_tot_psum w_inv_ready w_t_ready tern_ready")
        sgu, ssg, sh, sht_psum, sht, sy = named("sh_gu_ready sh_sg_ready sh_h_ready sh_ht_psum sh_ht_ready sh_y_done")
        base_ready, chosen_ready, rank_psum, place_ready, tile_e_ready, tile_e_psum, expert_ready, tile8_ready, hot_tile_ready, hot_ready, hot_used, now_ready, now_seen, slots_ready = named(
            "base_ready chosen_ready rank_psum place_ready tile_e_ready tile_e_psum expert_ready tile8_ready hot_tile_ready hot_ready hot_used now_ready now_seen slots_ready")
        xa_psum, xgT_ready, gu_ready, sg_ready, h_ready, ht_psum, ht_ready, y_psum, y_copied = named(
            "xa_psum xgT_ready gu_ready sg_ready h_ready ht_psum ht_ready y_psum y_copied")
        fetch_ready, xc_psum, xcT_ready, hd_psum = named("fetch_ready xc_psum xcT_ready hd_psum")
        qs1_ready, q1t_ready, q1_ready, q1T_psum, q1T_ready = named("qs1_ready q1t_ready q1_ready q1T_psum q1T_ready")
        up_psum, r_ready, r2_ready, mixed_ready, f_psum = named("up_psum r_ready r2_ready mixed_ready f_psum")
        qs2_ready, q2t_ready, q2_ready, q2T_psum, q2T_ready, d_psum, final_ready = named(
            "qs2_ready q2t_ready q2_ready q2T_psum q2T_ready d_psum final_ready")
        x_added = named("x_added_even x_added_odd")
        dve_chain = sem("dve_chain")

        block = ctx.enter_context(nc.Block())
        SH = SHARED * NPAIR
        WCHUNK = 4
        K_POOL = 2
        flat2 = "p t c -> p (t c)"

        @block.sync
        def _(sp):
            sp.dma_start(cst[:, :], consts).then_inc(cst_in, 16)
            sp.dma_start(subj[:, :], subj_rows).then_inc(small_in, 16)
            sp.dma_start(bias_s[:, :], bias).then_inc(small_in, 16)
            sp.dma_start(cond_w[:, :, :, :], cond).then_inc(small_in, 16)
            sp.dma_start(X[:, :, :], x).then_inc(x_in, 16)
            sp.dma_start(gate_s[:, :, :], gate).then_inc(gate_in, 16)
            sp.dma_start(W[:, E:EA, :], experts[E:EA].rearrange("e p c -> p e c")).then_inc(sw_in, 16)
            sp.dma_start(up_s, w_up).then_inc(wq_in, 16)
            sp.dma_start(down_s, w_down).then_inc(wq_in, 16)
            sp.wait_ge(rows_ready, NT)
            sp.dma_start(xf_dram.rearrange("(i p) d -> p i d", p=P), rows).then_inc(xf_out, 16)
            for e in range(0, E, WCHUNK):
                sp.dma_start(W[:, e:e + WCHUNK, :], experts[e:e + WCHUNK].rearrange("e p c -> p e c")).then_inc(w_in, 16)

            def store(s0, u, s):
                sp.wait_ge(y_copied, s0 + (u + 1))
                sp.dma_start(y_rows[:, s, :], yv[:, u, :]).then_inc(y_out[u], 16)

            y_rows = y_dram.rearrange("(p s t) d -> p s (t d)", p=P, t=2)
            for u in range(UNROLL):
                store(0, u, u)
            with sp.Fori(1, ROUNDS) as it:
                for u in range(UNROLL):
                    sp.wait_ge(y_copied, it * UNROLL + (u + 1))
                    sp.dma_start(y_rows[:, bass.ds(it * UNROLL + u, 1), :].rearrange("p a c -> p (a c)"), yv[:, u, :]
                                 ).then_inc(y_out[u], 16)
            for g, (i0, n) in enumerate(TAIL):
                sp.wait_ge(final_ready, g + 1)
                sp.dma_start(out[i0:i0 + n].rearrange("i p d -> p i d"), X[:, i0:i0 + n, :]).then_inc(out_done, 16)
            sp.wait_ge(out_done, 16 * len(TAIL))

        @block.gpsimd
        def _(pool):
            nc.gpsimd.memset(ones[:, :], 1.0)
            nc.gpsimd.memset(onesb[:, :], 1.0)
            nc.gpsimd.memset(magic[:, :], MAGIC)
            nc.gpsimd.memset(gmax[:, :, GROUPS:], -1.0)
            pool.wait_ge(cst_in, 16)
            nc.gpsimd.tensor_copy(identb[:, :], ident)
            nc.gpsimd.tensor_copy(lowerb[:, :], lower)
            nc.gpsimd.tensor_copy(iota16[:, :], iota).then_inc(filled, 1)

            def gather(s0, u):
                nc.gpsimd.tensor_copy(now[:, u, :], slot_token[:, bass.ds(s0 * 2 + 2 * u, 2)]).then_inc(now_ready, 1)
                pool.wait_ge(now_ready, s0 + (u + 1))
                pool.sem_inc(now_seen, 1)
                for t in range(2):
                    nc.gpsimd.indirect_dma_start(xg[:, u, t, :], None, xf_dram,
                                                 bass.IndirectOffsetOnAxis(now[:, u, t:t + 1], 0)).then_inc(xg_in[u], 16)

            pool.wait_ge(tile8_ready, 1)
            for i in range(NT):
                if i >= HOT:
                    pool.wait_ge(hot_used, i + 1 - HOT)
                for k in range(TOPK - K_POOL, TOPK):
                    ins = nc.gpsimd.tensor_scalar(hot_tile[:, i % HOT, k, :], iota16[:, 0:TILES], tile8[:, i, k:k + 1], token[:, i:i + 1],
                                                  ALU.is_equal, ALU.mult)
                ins.then_inc(hot_tile_ready, 1)
            pool.wait_ge(xf_out, 16)
            pool.wait_ge(slots_ready, 1)
            for u in range(UNROLL):
                gather(0, u)
            with pool.Fori(1, ROUNDS) as it:
                for u in range(UNROLL):
                    pool.wait_ge(xa_psum, it * UNROLL + (u + 1 - UNROLL))
                    gather(it * UNROLL, u)
            pool.wait_ge(fetch_ready, 1)
            for u in range(UNROLL):
                pool.wait_ge(y_out[u], 16 * ROUNDS)
            for g, (i0, n) in enumerate(TAIL):
                for k in range(TOPK):
                    for i in range(i0, i0 + n):
                        nc.gpsimd.indirect_dma_start(yg[:, i, k, :], None, y_dram,
                                                     bass.IndirectOffsetOnAxis(fetch[:, i, k:k + 1], 0)).then_inc(yg_in[g][k], 16)

        def halfbank(b):
            return ps[:, b, :].rearrange("p (t c) -> p t c", t=2)

        @block.tensor
        def _(pe):
            T = nc.tensor
            pe.wait_ge(x_in, 16)
            for i in range(NT):
                pe.wait_ge(cond_ready, i // 2 + 1)
                T.matmul(halfbank(i // 2)[:, i % 2, :], cond_bd[:, 0, i, :], X[:, i, :], start=True, stop=True).then_inc(rows_psum, 1)
            pe.wait_ge(filled, 1)
            for q in range(NPAIR):
                pe.wait_ge(rows_ready, 2 * q + 2)
                if q >= 2:
                    pe.wait_ge(xT_ready, q - 1)
                for t in range(2):
                    for k in range(KD):
                        at = k * 256 + t * P
                        mm = T.transpose(ps[:, 4 + q % 2, at:at + P], rows[:, 2 * q + t, k * P:(k + 1) * P], ident)
                mm.then_inc(xT_psum, 1)
            pe.wait_ge(gate_in, 16)
            for i in range(NT):
                pe.wait_ge(xT_ready, i // 2 + 1)
                for k in range(KD):
                    mm = T.matmul(ps[:, 7, i * E:(i + 1) * E], xT[:, k, i * P:(i + 1) * P], gate_s[:, k, :],
                                  start=(k == 0), stop=(k == KD - 1))
            mm.then_inc(logits_psum, 1)
            def sh_gate_up(s):
                e, q = E + s // NPAIR, s % NPAIR
                if s >= 2:
                    pe.wait_ge(sh, s - 1)
                for t in range(2):
                    i = 2 * q + t
                    for k in range(KD):
                        mm = T.matmul(halfbank(4 + s % 2)[:, t, :], xT[:, k, i * P:(i + 1) * P],
                                      W[:, e, k * 256:(k + 1) * 256], start=(k == 0), stop=(k == KD - 1))
                mm.then_inc(sgu, 1)

            def sh_turn(s):
                pe.wait_ge(sh, s + 1)
                for t in range(2):
                    mm = T.transpose(ps[:, 6, t * P:(t + 1) * P], h[:, s % 2, t, :], ident)
                mm.then_inc(sht_psum, 1)

            def sh_down(s):
                e, q = E + s // NPAIR, s % NPAIR
                if e == E:
                    T.matmul(ps[:, q, :], ident, X[:, 2 * q:2 * q + 2, :].rearrange(flat2),
                             start=True, stop=False, skip_group_check=True)
                pe.wait_ge(sht, s + 1)
                for t in range(2):
                    mm = T.matmul(halfbank(q)[:, t, :], hT[:, s % 2, t * P:(t + 1) * P], W[:, e, 512:512 + D],
                                  start=False, stop=(e == EA - 1), skip_group_check=True)
                mm.then_inc(sy, 1)

            def ranks():
                pe.wait_ge(w_abs_ready, 1)
                pe.wait_ge(chosen_ready, 1)
                T.matmul(ps[:, 7, 240:242], ones[:, :], w_abs[:, :], start=True, stop=True).then_inc(w_tot_psum, 1)
                T.matmul(ps[:, 7, 256:512], lowerb[:, :], chosen[:, :, :].rearrange("p i e -> p (i e)"), start=True, stop=False)
                for j in range(NT - 1):
                    mm = T.matmul(ps[:, 7, 256 + (j + 1) * E:512].rearrange("p (i e) -> p i e", e=E), onesb[:, :],
                                  chosen[:, j, :].unsqueeze(1).broadcast_to([P, NT - 1 - j, E]),
                                  start=False, stop=(j == NT - 2))
                for j in range(NT):
                    mm = T.matmul(ps[:, 7, 0:E], onesb[:, :], chosen[:, j, :], start=(j == 0), stop=(j == NT - 1))
                mm.then_inc(rank_psum, 1)

            def tile_experts():
                pe.wait_ge(tile_e_ready, 1)
                pe.wait_ge(place_ready, 1)
                T.matmul(ps[0:1, 7, 64:64 + TILES], tile_e[:, :], ident[:, 0:TILES], start=True, stop=True).then_inc(tile_e_psum, 1)

            def invert(i):
                pe.wait_ge(hot_ready, i + 1)
                pe.wait_ge(hot_tile_ready, i + 1)
                pe.wait_ge(expert_ready, 1)
                for k in range(TOPK):
                    mm = T.matmul(ps[:, 7, 160:160 + TILES], hot_row[:, i % HOT, k, :], hot_tile[:, i % HOT, k, :],
                                  start=(i == 0 and k == 0), stop=(i == NT - 1 and k == TOPK - 1))
                mm.then_inc(hot_used, 1)

            pe.wait_ge(sw_in, 16)
            sh_gate_up(0)
            sh_gate_up(1)
            def sh_step(s):
                sh_turn(s)
                if s + 2 < SH:
                    sh_gate_up(s + 2)
                if s == 0:
                    ranks()
                if s == 1:
                    tile_experts()
                sh_down(s)

            INVERTED = {2: 1, 3: 3, 4: 6, 5: NT}
            i0 = 0
            for s in range(SH):
                sh_step(s)
                for i in range(i0, INVERTED.get(s, i0)):
                    invert(i)
                i0 = INVERTED.get(s, i0)

            def turn_in(s0, u):
                pe.wait_ge(xg_in[u % UNROLL], s0 * (32 // UNROLL) + 32 * (u // UNROLL + 1))
                for t in range(2):
                    for k in range(KD):
                        at = (2 * t + k) * P
                        mm = T.transpose(ps[:, u % 2, at:at + P], xg[:, u % UNROLL, t, k * P:(k + 1) * P], ident)
                mm.then_inc(xa_psum, 1)

            def experts_of(s0, steps):
                _, es = nc.values_load_multi_w_load_instructions(
                    expert_of[0:1, bass.ds(s0 * 2, 2 * steps)], engines=[mybir.EngineType.PE], min_val=0, max_val=E - 1,
                    skip_runtime_bounds_check_because="the row counts experts that end and is capped at E - 1")
                return es

            def gate_up(es, s0, u):
                pe.wait_ge(xgT_ready, s0 + (u + 1))
                for t, e in enumerate(es[2 * u:2 * u + 2]):
                    for k in range(KD):
                        mm = T.matmul(halfbank(2 + u % 2)[:, t, :], xgT[:, u % 2, t, k, :],
                                      W[:, bass.ds(e, 1), k * 256:(k + 1) * 256], start=(k == 0), stop=(k == KD - 1))
                mm.then_inc(gu_ready, 1)

            def turn(s0, u):
                pe.wait_ge(h_ready, s0 + (u + 1))
                for t in range(2):
                    mm = T.transpose(ps[:, 4 + u % 2, t * P:(t + 1) * P], h[:, u % 2, t, :], ident)
                mm.then_inc(ht_psum, 1)

            def down(es, s0, u, first=False):
                pe.wait_ge(ht_ready, s0 + (u + 1))
                if not first:
                    pe.wait_ge(y_copied, s0 + (u - 1))
                for t, e in enumerate(es[2 * u:2 * u + 2]):
                    mm = T.matmul(halfbank(6 + u % 2)[:, t, :], hT[:, u % 2, t * P:(t + 1) * P],
                                  W[:, bass.ds(e, 1), 512:512 + D], start=True, stop=True)
                mm.then_inc(y_psum, 1)

            def round_(s0, first=False, last=False):
                es = experts_of(s0, UNROLL if last else UNROLL + 2)
                for u in range(UNROLL):
                    if not last or u + 3 < UNROLL:
                        turn_in(s0, u + 3)
                    if not last or u + 2 < UNROLL:
                        gate_up(es, s0, u + 2)
                    if not last or u + 1 < UNROLL:
                        turn(s0, u + 1)
                    down(es, s0, u, first and u < 2)

            pe.wait_ge(expert_ready, 1)
            es = experts_of(0, 2)
            pe.wait_ge(slots_ready, 1)
            pe.wait_ge(base_ready, 2)
            turn_in(0, 0)
            turn_in(0, 1)
            pe.wait_ge(w_in, 16 * (E // WCHUNK))
            pe.wait_ge(base_ready, NPAIR)
            gate_up(es, 0, 0)
            turn_in(0, 2)
            gate_up(es, 0, 1)
            turn(0, 0)
            round_(0, first=True)
            with pe.Fori(1, ROUNDS - 1) as it:
                round_(it * UNROLL)
            round_(STEPS - UNROLL, last=True)


            def condition1(g):
                i0, n = TAIL[g]
                for i in range(i0, i0 + n):
                    pe.wait_ge(x_added[i % 2], (i // 2 + 1) * TOPK)
                if g >= 1:
                    pe.wait_ge(q1T_ready, g)
                for t in range(n):
                    for a in range(KD):
                        at = a * 256 + t * P
                        mm = T.matmul(ps[:, 0, at:at + P], X[:, i0 + t, a * P:(a + 1) * P], cond_bd[:, 1, i0 + t, :],
                                      start=True, stop=True)
                mm.then_inc(xc_psum, 1)

            def hadamard1(g):
                i0, n = TAIL[g]
                pe.wait_ge(xcT_ready, g + 1)
                if g >= 1:
                    pe.wait_ge(q1t_ready, g)
                for t in range(n):
                    for a in range(KD):
                        mm = T.matmul(halfbank(1)[:, t, :], xcT[:, a, (i0 + t) * P:(i0 + t + 1) * P], had_rows[a],
                                      start=(a == 0), stop=(a == KD - 1))
                mm.then_inc(hd_psum, 1)

            def turn1(g):
                i0, n = TAIL[g]
                pe.wait_ge(q1_ready, g + 1)
                bank = ps[:, 0, :].bitcast(BF16)
                for t in range(n):
                    for k in range(KD):
                        at = k * 256 + t * P
                        mm = T.transpose(bank[:, at:at + P], q1[:, i0 + t, k * P:(k + 1) * P], identb[:, :])
                mm.then_inc(q1T_psum, 1)

            def up(g):
                i0, n = TAIL[g]
                pe.wait_ge(q1T_ready, g + 1)
                if g >= 1:
                    pe.wait_ge(r_ready, g)
                for m in range(KU):
                    for k in range(KD):
                        mm = T.matmul(halfbank(2 + m // 2)[:, m % 2, 0:n * P], tern[:, 0, k * UP + m * P:k * UP + (m + 1) * P],
                                      q1T[:, k, i0 * P:(i0 + n) * P], start=(k == 0), stop=(k == KD - 1))
                mm.then_inc(up_psum, 1)

            def hadamard2(g):
                pe.wait_ge(mixed_ready, g + 1)
                if g >= 1:
                    pe.wait_ge(q2t_ready, g)
                for t in range(TAIL[g][1]):
                    for a in range(KU):
                        mm = T.matmul(ps[:, 4 + t, a * P:(a + 1) * P], r4[:, a, t * P:(t + 1) * P], had, start=True, stop=True)
                mm.then_inc(f_psum, 1)

            def turn2(g):
                pe.wait_ge(q2_ready, g + 1)
                bank = ps[:, 6, :].bitcast(BF16)
                for t in range(TAIL[g][1]):
                    for a in range(KU):
                        at = (t * KU + a) * P
                        mm = T.transpose(bank[:, at:at + P], q2[:, t, a * P:(a + 1) * P], identb[:, :])
                mm.then_inc(q2T_psum, 1)

            def down2(g):
                pe.wait_ge(q2T_ready, g + 1)
                if g >= 1:
                    pe.wait_ge(final_ready, g)
                for t in range(TAIL[g][1]):
                    for a in range(KU):
                        mm = T.matmul(halfbank(7)[:, t, :], q2T[:, t, a * P:(a + 1) * P], tern[:, 1, a * D:(a + 1) * D],
                                      start=(a == 0), stop=(a == KU - 1))
                mm.then_inc(d_psum, 1)

            pe.wait_ge(cond_ready, NPAIR + 1)
            pe.wait_ge(y_copied, STEPS)
            pe.wait_ge(tern_ready, 1)
            for g in range(len(TAIL) + 2):
                if g < len(TAIL):
                    condition1(g)
                if g >= 2:
                    down2(g - 2)
                if g < len(TAIL):
                    hadamard1(g)
                if 1 <= g <= len(TAIL):
                    hadamard2(g - 1)
                if g < len(TAIL):
                    turn1(g)
                    up(g)
                if 1 <= g <= len(TAIL):
                    turn2(g - 1)

        @block.scalar
        def _(act):
            A = nc.scalar
            for i in range(NT):
                act.wait_ge(rows_psum, i // 2 * 2 + 2)
                A.activation(rows[:, i, :], halfbank(i // 2)[:, i % 2, :], ACT.Identity, bias=bias_row[:, i:i + 1]
                             ).then_inc(rows_ready, 1)
            act.wait_ge(logits_psum, 1)
            A.activation(scores[:, :, :].rearrange("p i e -> p (i e)"), ps[:, 7, 0:NT * E], ACT.Sigmoid).then_inc(scores_ready, 1)

            def sh_silu(s):
                act.wait_ge(sgu, s + 1)
                A.activation(sg[:, s % 2, :, :], halfbank(4 + s % 2)[:, :, 0:INTER], ACT.Silu).then_inc(ssg, 1)

            def base(q):
                act.wait_ge(sy, SH - NPAIR + q + 1)
                A.copy(X[:, 2 * q:2 * q + 2, :].rearrange(flat2), ps[:, q, :]).then_inc(base_ready, 1)

            sh_silu(0)
            for s in range(SH):
                if s + 1 < SH:
                    sh_silu(s + 1)
                act.wait_ge(sht_psum, s + 1)
                A.copy(hT[:, s % 2, :], ps[:, 6, 0:256]).then_inc(sht, 1)
                if s > NPAIR:
                    base(s - 1 - NPAIR)
            base(NPAIR - 1)

            def copy_in(s0, u):
                act.wait_ge(xa_psum, s0 + (u + 1))
                A.copy(xgT_area[:, u % 2 * 512:(u % 2 + 1) * 512], ps[:, u % 2, :]).then_inc(xgT_ready, 1)

            def silu(s0, u):
                act.wait_ge(gu_ready, s0 + (u + 1))
                A.activation(sg[:, u % 2, :, :], halfbank(2 + u % 2)[:, :, 0:INTER], ACT.Silu).then_inc(sg_ready, 1)

            def copy_h(s0, u):
                act.wait_ge(ht_psum, s0 + (u + 1))
                A.copy(hT[:, u % 2, :], ps[:, 4 + u % 2, 0:256]).then_inc(ht_ready, 1)

            def round_(s0, last=False):
                for u in range(UNROLL):
                    if not last or u + 3 < UNROLL:
                        copy_in(s0, u + 3)
                    if not last or u + 2 < UNROLL:
                        silu(s0, u + 2)
                    if not last or u + 1 < UNROLL:
                        copy_h(s0, u + 1)

            copy_in(0, 0)
            copy_in(0, 1)
            silu(0, 0)
            copy_in(0, 2)
            silu(0, 1)
            copy_h(0, 0)
            with act.Fori(0, ROUNDS - 1) as it:
                round_(it * UNROLL)
            round_(STEPS - UNROLL, last=True)


            act.wait_ge(w_inv_ready, 1)
            for n, w in enumerate((up_s, down_s)):
                ins = A.activation(w_t[:, n, :], w, ACT.Identity, bias=magic[:, :], scale=w_inv[:, n:n + 1])
            ins.then_inc(w_t_ready, 1)

            def copy_xc(g):
                i0, n = TAIL[g]
                act.wait_ge(xc_psum, g + 1)
                A.copy(xcT[:, :, i0 * P:(i0 + n) * P], halfbank(0)[:, :, 0:n * P]).then_inc(xcT_ready, 1)

            def round1(g):
                i0, n = TAIL[g]
                act.wait_ge(qs1_ready, g + 1)
                for t in range(n):
                    ins = A.activation(q1t[:, i0 + t, :], halfbank(1)[:, t, :], ACT.Identity,
                                       bias=magic[:, :], scale=qs1[:, i0 + t:i0 + t + 1])
                ins.then_inc(q1t_ready, 1)

            def copy_q1(g):
                i0, n = TAIL[g]
                act.wait_ge(q1T_psum, g + 1)
                A.copy(q1T[:, :, i0 * P:(i0 + n) * P],
                       ps[:, 0, :].bitcast(BF16)[:, 0:512].rearrange("p (k n) -> p k n", k=KD)[:, :, 0:n * P]).then_inc(q1T_ready, 1)

            def squared_relu(g):
                cols = TAIL[g][1] * P
                act.wait_ge(up_psum, g + 1)
                if g >= 1:
                    act.wait_ge(mixed_ready, g)
                A.activation(r[:, :, 0:cols], ps[:, 2:4, :].rearrange("p b (m n) -> p (b m) n", m=2)[:, :, 0:cols], ACT.Relu
                             ).then_inc(r_ready, 1)
                act.wait_ge(r_ready, g + 1)
                A.activation(r2[:, :, 0:cols], r[:, :, 0:cols], ACT.Square).then_inc(r2_ready, 1)

            def round2(g):
                i0, n = TAIL[g]
                act.wait_ge(qs2_ready, g + 1)
                if g >= 1:
                    act.wait_ge(q2_ready, g)
                for t in range(n):
                    ins = A.activation(q2t[:, t, :], ps[:, 4 + t, :], ACT.Identity, bias=magic[:, :],
                                       scale=qs2[:, i0 + t:i0 + t + 1])
                ins.then_inc(q2t_ready, 1)

            def copy_q2(g):
                n = TAIL[g][1]
                act.wait_ge(q2T_psum, g + 1)
                if g >= 1:
                    act.wait_ge(d_psum, g)
                A.copy(q2T[:, 0:n, :].rearrange("p t c -> p (t c)"), ps[:, 6, :].bitcast(BF16)[:, 0:n * UP]).then_inc(q2T_ready, 1)

            for g in range(len(TAIL) + 2):
                if g >= 2:
                    copy_q2(g - 2)
                if g < len(TAIL):
                    copy_xc(g)
                    round1(g)
                    copy_q1(g)
                if 1 <= g <= len(TAIL):
                    round2(g - 1)
                if g < len(TAIL):
                    squared_relu(g)

        @block.vector
        def _(v):
            chained = [0]

            def link(ins):
                chained[0] += 1
                ins.then_inc(dve_chain, 1)
                v.wait_ge(dve_chain, chained[0])

            V = nc.vector

            def bc(ap, dims, shape):
                for d in dims:
                    ap = ap.unsqueeze(d)
                return ap.broadcast_to(shape)

            v.wait_ge(cst_in, 16)
            v.wait_ge(small_in, 48)
            link(V.tensor_copy(subj_f[:, :], subj[:, :]))
            link(V.tensor_tensor(subj_mask[:, :, :], bc(subj_f[:, :], [2], [P, NT, SUBJ]), bc(iota[:, 0:SUBJ], [1], [P, NT, SUBJ]),
                                 ALU.is_equal))
            link(V.tensor_tensor(bias_t[:, :, :], bc(bias_s[:, :], [1], [P, NT, SUBJ]), subj_mask[:, :, :], ALU.mult))
            V.tensor_reduce(bias_row[:, :], bias_t[:, :, :], AX.X, ALU.add)

            def spread(area):
                return area[:, :].rearrange("p (i n s) -> p i n s", i=NT, n=SUBJ)

            def condition(layer, cond_t, i0, n):
                at = slice(i0, i0 + n)
                link(V.tensor_tensor(cond_t[:, at, :, :], bc(cond_w[:, layer, :, :], [1], [P, n, SUBJ, S]),
                                     bc(subj_mask[:, at, :], [3], [P, n, SUBJ, S]), ALU.mult))
                link(V.tensor_reduce(cond_sel[:, layer, at, :], cond_t[:, at, :, :].rearrange("p i n s -> p i s n"), AX.X, ALU.add))
                V.tensor_tensor(cond_bd[:, layer, at, :].rearrange("p i (j s) -> p i j s", j=BPT),
                                bc(cond_sel[:, layer, at, :], [2], [P, n, BPT, S]),
                                bc(bc(diag, [1], [P, n, BPT]), [3], [P, n, BPT, S]), ALU.mult).then_inc(cond_ready, 1)

            for i in range(0, NT, 2):
                condition(0, spread(y_area), i, 2)
            for q in range(NPAIR):
                v.wait_ge(xT_psum, q + 1)
                V.tensor_copy(xT[:, :, q * 256:(q + 1) * 256], ps[:, 4 + q % 2, :].rearrange("p (k n) -> p k n", k=KD)
                              ).then_inc(xT_ready, 1)
            v.wait_ge(wq_in, 32)
            V.tensor_reduce(w_abs[:, 0:1], up_s, AX.X, ALU.add, apply_absolute_value=True)
            V.tensor_reduce(w_abs[:, 1:2], down_s, AX.X, ALU.add, apply_absolute_value=True).then_inc(w_abs_ready, 1)

            def sh_mul(s):
                v.wait_ge(ssg, s + 1)
                if s >= 2:
                    v.wait_ge(sht_psum, s - 1)
                V.tensor_tensor(h[:, s % 2, :, :], sg[:, s % 2, :, :], halfbank(4 + s % 2)[:, :, INTER:], ALU.mult).then_inc(sh, 1)

            groups = [P, NT, GROUPS, E // GROUPS]

            def grouped(t):
                return t[:, :, :].rearrange("p i (g m) -> p i g m", g=GROUPS)

            v.wait_ge(scores_ready, 1)
            link(V.tensor_reduce(gmax[:, :, 0:GROUPS], grouped(scores), AX.X, ALU.max))
            for i in range(NT):
                ins = V.max(gtop[:, i, :], gmax[:, i, 0:GROUPS])
            link(ins)
            link(V.memset(gtop[:, :, TOPK_G:], -1.0))
            for i in range(NT):
                ins = V.match_replace(grep[:, i, :], gtop[:, i, :], gmax[:, i, :], -2.0)
            link(ins)
            link(V.tensor_scalar(gmask[:, :, :], grep[:, :, 0:GROUPS], 0.0, None, ALU.is_lt))
            link(V.tensor_tensor(grouped(smask), grouped(scores), bc(gmask[:, :, :], [3], groups), ALU.mult))
            link(V.tensor_scalar(gmask[:, :, :], gmask[:, :, :], 1.0, None, ALU.subtract))
            sh_mul(0)
            link(V.tensor_tensor(grouped(smask), grouped(smask), bc(gmask[:, :, :], [3], groups), ALU.add))
            for i in range(NT):
                ins = V.max(stop8[:, i, :], smask[:, i, :])
            link(ins)
            link(V.memset(stop8[:, :, TOPK:], -1.0))
            for i in range(NT):
                ins = V.match_replace(srep[:, i, :], stop8[:, i, :], smask[:, i, :], -2.0)
            link(ins)
            link(V.tensor_scalar(smask[:, :, :], smask[:, :, :], 0.0, None, ALU.is_ge))
            V.scalar_tensor_tensor(chosen[:, :, :], srep[:, :, :], 0.0, smask[:, :, :], ALU.is_lt, ALU.mult).then_inc(chosen_ready, 1)
            v.wait_ge(chosen_ready, 1)
            sh_mul(1)
            v.wait_ge(rank_psum, 1)
            link(V.tensor_scalar(tiles_of[:, :], ps[:, 7, 0:E], 1.0 / P, 0.5 - 0.5 / P, ALU.mult, ALU.add))
            link(V.tensor_scalar(tiles_of[:, :], tiles_of[:, :], MAGIC, MAGIC, ALU.add, ALU.subtract))
            link(V.tensor_tensor_scan(tiles_end[:, :], ones[:, 0:E], tiles_of[:, :], 0.0, ALU.mult, ALU.add))
            link(V.tensor_tensor(tiles_from[:, :], tiles_end[:, :], tiles_of[:, :], ALU.subtract))
            v.wait_ge(w_tot_psum, 1)
            V.tensor_scalar(w_tot[:, :], ps[:, 7, 240:242], 1.0 / (UP * D), EPS, ALU.mult, ALU.max)
            link(V.tensor_scalar(begun[:, :], tiles_end[:, :], token[:, 0:1], None, ALU.is_le))
            V.tensor_reduce(tile_e[:, :], begun[:, :], AX.X, ALU.add).then_inc(tile_e_ready, 1)
            rank = ps[:, 7, 256:512].rearrange("p (i e) -> p i e", e=E)
            link(V.tensor_scalar(turnover[:, :, :], rank, 1.0 / P, 0.5 / P - 0.5, ALU.mult, ALU.add))
            link(V.tensor_scalar(turnover[:, :, :], turnover[:, :, :], MAGIC, MAGIC, ALU.add, ALU.subtract))
            link(V.scalar_tensor_tensor(turnover[:, :, :], turnover[:, :, :], 1.0 - P * TILES,
                                        bc(tiles_from[:, :], [1], [P, NT, E]), ALU.mult, ALU.add))
            V.scalar_tensor_tensor(place[:, :, :], rank, float(TILES), turnover[:, :, :], ALU.mult, ALU.add).then_inc(place_ready, 1)
            v.wait_ge(place_ready, 1)
            link(V.scalar_tensor_tensor(place[:, :, :], place[:, :, :], 1.0, chosen[:, :, :], ALU.add, ALU.mult))
            sh_mul(2)
            for i in range(NT):
                ins = V.max(place8[:, i, :], place[:, i, :])
            link(ins)
            link(V.tensor_scalar(part8[:, :, :], place8[:, :, :], 1.0 / TILES, -0.5 - 0.5 / TILES, ALU.mult, ALU.add))
            link(V.tensor_scalar(part8[:, :, :], part8[:, :, :], MAGIC, MAGIC, ALU.add, ALU.subtract))
            link(V.scalar_tensor_tensor(tile8[:, :, :], part8[:, :, :], -float(TILES), place8[:, :, :], ALU.mult, ALU.add))
            V.tensor_scalar(tile8[:, :, :], tile8[:, :, :], 1.0, None, ALU.subtract).then_inc(tile8_ready, 1)
            V.reciprocal(w_inv[:, :], w_tot[:, :]).then_inc(w_inv_ready, 1)
            V.tensor_scalar(w_up_scaled[:, :], w_tot[:, 0:1], float(D) ** -0.5, None, ALU.mult)
            v.wait_ge(tile8_ready, 1)
            v.wait_ge(tile_e_psum, 1)
            V.tensor_scalar(expert_of[:, :], ps[0:1, 7, 64:64 + TILES], float(E - 1), None, ALU.min).then_inc(expert_ready, 1)

            def one_hot(i):
                if i >= HOT:
                    v.wait_ge(hot_used, i + 1 - HOT)
                for k in range(TOPK):
                    ins = V.tensor_scalar(hot_row[:, i % HOT, k, :], iota16[:, :], part8[:, i, k:k + 1], None, ALU.is_equal)
                for k in range(TOPK - K_POOL):
                    ins = V.tensor_scalar(hot_tile[:, i % HOT, k, :], iota16[:, 0:TILES], tile8[:, i, k:k + 1], token[:, i:i + 1],
                                          ALU.is_equal, ALU.mult)
                ins.then_inc(hot_ready, 1)

            for i in range(NT):
                one_hot(i)
                if i in (0, 2, 5):
                    sh_mul(3 + i // 2)
            v.wait_ge(hot_used, NT)
            V.tensor_copy(slot_token[:, :], ps[:, 7, 160:160 + TILES]).then_inc(slots_ready, 1)
            sh_mul(6)
            sh_mul(7)
            link(V.tensor_tensor(scores[:, :, :], scores[:, :, :], chosen[:, :, :], ALU.mult))
            link(V.tensor_reduce(wsum[:, :], scores[:, :, :], AX.X, ALU.add))
            link(V.reciprocal(wrec[:, :], wsum[:, :]))
            link(V.scalar_tensor_tensor(scores[:, :, :], scores[:, :, :], ROUTE_SCALE, bc(wrec[:, :], [2], [P, NT, E]),
                                        ALU.mult, ALU.mult))
            V.tensor_scalar(fetch[:, :, :], place8[:, :, :], 1.0, None, ALU.subtract).then_inc(fetch_ready, 1)
            each = [P, NT, TOPK, E]
            link(V.tensor_tensor(match, bc(place8[:, :, 0:TOPK], [3], each), bc(place[:, :, :], [2], each), ALU.is_equal))
            link(V.tensor_tensor(match, match, bc(scores[:, :, :], [2], each), ALU.mult))
            link(V.tensor_reduce(weight[:, :, :], match, AX.X, ALU.add))

            def mul(s0, u):
                v.wait_ge(sg_ready, s0 + (u + 1))
                V.tensor_tensor(h[:, u % 2, :, :], sg[:, u % 2, :, :], halfbank(2 + u % 2)[:, :, INTER:], ALU.mult).then_inc(h_ready, 1)

            def copy_y(s0, u, first=False):
                v.wait_ge(y_psum, s0 + (u + 1))
                if not first:
                    v.wait_ge(y_out[u], s0 * (16 // UNROLL))
                V.tensor_copy(yv[:, u, :], ps[:, 6 + u % 2, :]).then_inc(y_copied, 1)

            def round_(s0, first=False, last=False):
                for u in range(UNROLL):
                    if not last or u + 2 < UNROLL:
                        mul(s0, u + 2)
                    copy_y(s0, u, first)

            mul(0, 0)
            mul(0, 1)
            round_(0, first=True)
            with v.Fori(1, ROUNDS - 1) as it:
                round_(it * UNROLL)
            round_(STEPS - UNROLL, last=True)
            condition(1, spread(rows_area), 0, NT)
            v.wait_ge(w_t_ready, 1)
            link(V.tensor_scalar(w_c, w_t, MAGIC, 1.0, ALU.subtract, ALU.min))
            V.tensor_scalar(tern[:, :, :], w_c, -1.0, None, ALU.max).then_inc(tern_ready, 1)

            def combine(g, k):
                i0, n = TAIL[g]
                v.wait_ge(yg_in[g][k], 16 * n)
                for i in range(i0, i0 + n):
                    if k:
                        v.wait_ge(x_added[i % 2], k + i // 2 * TOPK)
                    ins = V.scalar_tensor_tensor(X[:, i, :], yg[:, i, k, :], weight[:, i, k:k + 1], X[:, i, :], ALU.mult, ALU.add
                                                 ).then_inc(x_added[i % 2], 1)

            def stats1(g):
                i0, n = TAIL[g]
                v.wait_ge(hd_psum, g + 1)
                at = slice(i0, i0 + n)
                link(V.tensor_reduce(amax1[:, at], halfbank(1)[:, 0:n, :], AX.X, ALU.max, apply_absolute_value=True))
                link(V.tensor_scalar(m1[:, at], amax1[:, at], EPS * float(D) ** 0.5, 1.0 / QMAX, ALU.max, ALU.mult))
                V.reciprocal(qs1[:, at], m1[:, at]).then_inc(qs1_ready, 1)

            def factors1(g):
                i0, n = TAIL[g]
                at = slice(i0, i0 + n)
                link(V.tensor_scalar(f1[:, at], m1[:, at], w_up_scaled[:, :], None, ALU.mult))
                link(V.scalar_tensor_tensor(fsq[:, at], f1[:, at], float(UP) ** -0.5, f1[:, at], ALU.mult, ALU.mult))
                link(V.reciprocal(guard2[:, at], fsq[:, at]))
                V.tensor_scalar(guard2[:, at], guard2[:, at], EPS / QMAX, None, ALU.mult)

            def clip1(g):
                i0, n = TAIL[g]
                v.wait_ge(q1t_ready, g + 1)
                at = slice(i0, i0 + n)
                link(V.tensor_scalar(q1c[:, at, :], q1t[:, at, :], MAGIC, QMAX, ALU.subtract, ALU.min))
                V.tensor_scalar(q1[:, at, :], q1c[:, at, :], -QMAX, None, ALU.max).then_inc(q1_ready, 1)

            def mix(g):
                cols = TAIL[g][1] * P
                a, b, c = (t.rearrange("p (c d) n -> p c d n", c=2)[:, :, :, 0:cols] for t in (r2, r3, r4))
                v.wait_ge(r2_ready, g + 1)
                V.tensor_tensor(b[:, :, 0, :], a[:, :, 0, :], a[:, :, 1, :], ALU.add)
                link(V.tensor_tensor(b[:, :, 1, :], a[:, :, 0, :], a[:, :, 1, :], ALU.subtract))
                if g >= 1:
                    v.wait_ge(f_psum, g)
                V.tensor_tensor(c[:, 0, :, :], b[:, 0, :, :], b[:, 1, :, :], ALU.add)
                V.tensor_tensor(c[:, 1, :, :], b[:, 0, :, :], b[:, 1, :, :], ALU.subtract).then_inc(mixed_ready, 1)

            def stats2(g):
                i0, n = TAIL[g]
                v.wait_ge(f_psum, g + 1)
                at = slice(i0, i0 + n)
                link(V.tensor_reduce(amax2[:, at], ps[:, 4:4 + n, :], AX.X, ALU.max, apply_absolute_value=True))
                link(V.scalar_tensor_tensor(m2[:, at], amax2[:, at], 1.0 / QMAX, guard2[:, at], ALU.mult, ALU.max))
                V.reciprocal(qs2[:, at], m2[:, at]).then_inc(qs2_ready, 1)
                V.scalar_tensor_tensor(f2[:, at], m2[:, at], w_tot[:, 1:2], fsq[:, at], ALU.mult, ALU.mult)

            def clip2(g):
                n = TAIL[g][1]
                v.wait_ge(q2t_ready, g + 1)
                link(V.tensor_scalar(q2c[:, 0:n, :], q2t[:, 0:n, :], MAGIC, QMAX, ALU.subtract, ALU.min))
                if g >= 1:
                    v.wait_ge(q2T_psum, g)
                V.tensor_scalar(q2[:, 0:n, :], q2c[:, 0:n, :], -QMAX, None, ALU.max).then_inc(q2_ready, 1)

            def final(g):
                i0, n = TAIL[g]
                v.wait_ge(d_psum, g + 1)
                for t in range(n):
                    ins = V.scalar_tensor_tensor(X[:, i0 + t, :], halfbank(7)[:, t, :], f2[:, i0 + t:i0 + t + 1], X[:, i0 + t, :],
                                                 ALU.mult, ALU.add)
                ins.then_inc(final_ready, 1)

            v.wait_ge(base_ready, NPAIR)
            G = len(TAIL)
            for g in range(G + 3):
                if g < G:
                    combine(g, 0)
                if 2 <= g < G + 2:
                    mix(g - 2)
                if g < G:
                    combine(g, 1)
                if g >= 3:
                    final(g - 3)
                if 1 <= g < G + 1:
                    stats1(g - 1)
                if g < G:
                    combine(g, 2)
                if 2 <= g < G + 2:
                    stats2(g - 2)
                if 1 <= g < G + 1:
                    clip1(g - 1)
                    factors1(g - 1)
                if g < G:
                    combine(g, 3)
                    combine(g, 4)
                if 2 <= g < G + 2:
                    clip2(g - 2)
                if g < G:
                    combine(g, 5)


def hadamard(n):
    m = np.ones((1, 1), np.float32)
    while m.shape[0] < n:
        m = np.block([[m, m], [m, -m]])
    return m


def constants():
    c = np.zeros((P, C_END), np.float32)
    c[:, C_ID:C_ID + P] = np.eye(P)
    c[:, C_HAD:C_HAD + 3 * P] = np.concatenate([hadamard(P), hadamard(P), -hadamard(P)], 1)
    c[:, C_LOWER:C_LOWER + P] = np.arange(P)[:, None] < np.arange(P)
    c[:, C_IOTA:C_IOTA + P] = np.arange(P)
    c[:, C_DIAG:C_DIAG + BPT] = np.arange(P)[:, None] // S == np.arange(BPT)
    c[:, C_TOKEN:C_TOKEN + NT] = np.arange(P)[:, None] + P * np.arange(NT)
    return c


def kernel(**inputs):
    import concourse.bacc as _bacc
    from concourse.bass_utils import run_bass_kernel_spmd as _run

    a = {k: np.asarray(v) for k, v in inputs.items()}
    subj = a["itok_B_0_7"]
    x = a["x"].reshape(NT, P, D).transpose(1, 0, 2)

    def cond(w):
        return np.tile(w.transpose(1, 0, 2), (BPT, 1, 1))

    def inward(w):
        t = np.swapaxes(w, -1, -2)
        t = t.reshape(*t.shape[:-2], KD, P, t.shape[-1])
        return np.swapaxes(t, -3, -2)

    def expert(w1, w3, w2):
        gu = np.concatenate([inward(w1), inward(w3)], -1).reshape(-1, P, KD * 2 * INTER)
        return np.concatenate([gu, np.swapaxes(w2, -1, -2)], -1)

    sw = [a["L0_ffn_sw1"].reshape(SHARED, INTER, D), a["L0_ffn_sw3"].reshape(SHARED, INTER, D),
          a["L0_ffn_sw2"].reshape(D, SHARED, INTER).transpose(1, 0, 2)]
    arrays = {
        "x": x,
        "subj_rows": np.repeat(subj.reshape(NT, BPT).T, S, axis=0),
        "bias": np.tile(a["fside_8xS_0"].T, (BPT, 1)),
        "gate": inward(a["L0_ffn_gate_w"]),
        "experts": np.concatenate([expert(a["L0_ffn_w11"], a["L0_ffn_w33"], a["L0_ffn_w22"]), expert(*sw)]),
        "cond": np.stack([cond(a["L0_cond_weights"]), cond(a["L1_cond_weights"])], 1),
        "w_up": inward(a["L1_ffn_w_up"]).reshape(P, KD * UP),
        "w_down": a["L1_ffn_w_down"].T.reshape(KU, P, D).transpose(1, 0, 2).reshape(P, KU * D),
        "consts": constants(),
    }
    arrays = {k: np.ascontiguousarray(v) for k, v in arrays.items()}
    nc = _bacc.Bacc("TRN2", target_bir_lowering=False, num_devices=1)
    aps = {k: nc.dram_tensor(f"in_{k}", v.shape, mybir.dt.from_np(v.dtype), kind="ExternalInput").ap() for k, v in arrays.items()}
    out = nc.dram_tensor("out_0", (NT, P, D), F32, kind="ExternalOutput").ap()
    xf_dram = nc.dram_tensor("xf_rows", (N, D), F32).ap()
    y_dram = nc.dram_tensor("y_rows", (P * TILES, D), F32).ap()
    build(nc, out=out, xf_dram=xf_dram, y_dram=y_dram, **aps)
    res = _run(nc, [{f"in_{k}": v for k, v in arrays.items()}], core_ids=[0])
    return res.results[0]["out_0"].reshape(B, S, D)
```

```python
from contextlib import ExitStack

import numpy as np

import concourse.bass as bass
from concourse import mybir

P = 128
B, S, D = 32, 32, 256
N = B * S
NT = N // P
NPAIR = NT // 2
BPT = P // S
KD = D // P
SUBJ = 8
E, INTER = 32, 128
GROUPS, TOPK_G, TOPK = 8, 4, 6
ROUTE_SCALE = 2.5
SHARED = 2
EA = E + SHARED
WCOLS = KD * 2 * INTER + D
TILES_MAX = N * TOPK // P + E - 1
TILES = -(-TILES_MAX // 8) * 8
UNROLL = 4
STEPS = TILES // 2
ROUNDS = STEPS // UNROLL
LAST_TILES = TILES_MAX - 2 * (STEPS - 1)
HOT = 4
UP = 512
KU = UP // P
QMAX = 127.0
EPS = 1e-5
MAGIC = 12582912.0

F32 = mybir.dt.float32
F16 = mybir.dt.float16
BF16 = mybir.dt.bfloat16
I32 = mybir.dt.int32
ALU = mybir.AluOpType
ACT = mybir.ActivationFunctionType
AX = mybir.AxisListType

C_ID = 0
C_HAD = C_ID + P
C_LOWER = C_HAD + 3 * P
C_IOTA = C_LOWER + P
C_DIAG = C_IOTA + P
C_TOKEN = C_DIAG + BPT
C_END = C_TOKEN + NT


def build(nc, x, subj_rows, bias, gate, experts, cond, w_up, w_down, consts, out, xf_dram, y_dram):
    ctx = ExitStack()
    with ctx:
        def sb(name, shape, dt=F32):
            return ctx.enter_context(nc.sbuf_tensor(name, shape, dt))

        def sem(name):
            return ctx.enter_context(nc.semaphore(name))

        ps = ctx.enter_context(nc.psum_tensor("ps", [P, 8, 512], F32))

        X = sb("X", [P, NT, D])
        cst = sb("cst", [P, C_END])
        ident, had, lower = (cst[:, c:c + P] for c in (C_ID, C_HAD, C_LOWER))
        had_rows = [cst[:, C_HAD + a * P:C_HAD + (a + 2) * P] for a in range(KD)]
        iota = cst[:, C_IOTA:C_IOTA + P]
        diag = cst[:, C_DIAG:C_DIAG + BPT]
        token = cst[:, C_TOKEN:C_TOKEN + NT]
        lowerb = sb("lowerb", [P, P], BF16)
        onesb = sb("onesb", [P, P], BF16)
        ones = sb("ones", [P, P])
        iota_k = sb("iota_k", [P, P, TOPK], F16)
        magic = sb("magic", [P, 1])
        neg_magic = sb("neg_magic", [P, 1])
        subj = sb("subj", [P, NT], I32)
        subj_f = sb("subj_f", [P, NT])
        subj_mask = sb("subj_mask", [P, NT, SUBJ])
        bias_s = sb("bias_s", [P, SUBJ])
        bias_t = sb("bias_t", [P, NT, SUBJ])
        bias_row = sb("bias_row", [P, NT])
        cond_w = sb("cond_w", [P, 2, SUBJ, S])
        cond_sel = sb("cond_sel", [P, 2, NT, S])
        cond_bd = sb("cond_bd", [P, 2, NT, P])
        gate_s = sb("gate_s", [P, KD, E])
        rows_area = sb("rows_area", [P, NT * D])
        rows = rows_area[:, :].rearrange("p (i d) -> p i d", i=NT)
        xcT = rows_area[:, :].rearrange("p (a n) -> p a n", a=KD)
        xT_area = sb("xT_area", [P, NT * D])
        xT = xT_area[:, :].rearrange("p (k n) -> p k n", k=KD)
        scores = sb("scores", [P, NT, E])
        gmax = sb("gmax", [P, NT, 2 * GROUPS])
        gtop = sb("gtop", [P, NT, 8])
        grep = sb("grep", [P, NT, 2 * GROUPS])
        gmask = sb("gmask", [P, NT, GROUPS])
        smask = sb("smask", [P, NT, E])
        stop8 = sb("stop8", [P, NT, 8])
        srep = sb("srep", [P, NT, E])
        chosen = sb("chosen", [P, NT, E], BF16)
        wsum = sb("wsum", [P, NT])
        wrec = sb("wrec", [P, NT])
        tiles_of = sb("tiles_of", [P, E])
        tiles_end = sb("tiles_end", [P, E])
        tiles_from = sb("tiles_from", [P, E])
        begun = sb("begun", [P, E])
        tile_e = sb("tile_e", [P, 1])
        expert_of = sb("expert_of", [1, TILES], I32)
        turnover = srep
        place = sb("place", [P, NT, E])
        place8 = sb("place8", [P, NT, 8])
        part8 = sb("part8", [P, NT, 8], F16)
        tile8 = sb("tile8", [P, NT, 8], F16)
        turn8 = sb("turn8", [P, NT, 8])
        fetch = sb("fetch", [P, NT, 8], I32)
        weight = sb("weight", [P, NT, TOPK])
        slot_token = sb("slot_token", [P, TILES], I32)
        now = sb("now", [P, UNROLL, 2], I32)
        W = sb("W", [P, EA, WCOLS])
        wflat = W[:, :, :].rearrange("p e c -> p (e c)")
        YG, NR = NT * TOPK * D, UP
        yg = wflat[:, 0:YG].rearrange("p (i k d) -> p i k d", i=NT, k=TOPK)
        r, r2, r3, r4 = (
            [wflat[:, YG + n * NR:YG + (n + 1) * NR].rearrange("p (m n) -> p m n", m=KU) for n in (2 * m, 2 * m + 1)]
            for m in range(4))
        DG = YG + 8 * NR
        diag_w = wflat[:, DG:DG + NT * TOPK * P].rearrange("p (i k c) -> p i k c", i=NT, k=TOPK)
        sg = sb("sg", [P, 2, 2, INTER])
        h = sb("h", [P, 2, 2, P])
        xg_area = sb("xg_area", [P, UNROLL * 2 * D])
        xg = xg_area[:, :].rearrange("p (u t d) -> p u t d", u=UNROLL, t=2)
        xgT_area = sb("xgT_area", [P, 2 * 512])
        xgT = xgT_area[:, :].rearrange("p (u t k n) -> p u t k n", u=2, t=2, k=KD)
        q1T = xgT_area[:, :].bitcast(BF16).rearrange("p (k n) -> p k n", k=KD)
        y_area = sb("y_area", [P, UNROLL * 2 * D])
        yv = y_area[:, :].rearrange("p (u c) -> p u c", u=UNROLL)
        match = rows_area[:, 0:NT * TOPK * E].rearrange("p (i k e) -> p i k e", i=NT, k=TOPK)
        hot_row = y_area[:, 0:HOT * TOPK * P // 2].bitcast(F16).rearrange("p (r c k) -> p r c k", r=HOT, k=TOPK)
        HT = HOT * TOPK * TILES // 2
        hot_tile, token_tile = (xg_area[:, n * HT:(n + 1) * HT].bitcast(F16).rearrange("p (r c k) -> p r c k", r=HOT, k=TOPK)
                                for n in range(2))
        wq_area = sb("wq_area", [P, 2048])
        up_s, down_s = wq_area[:, 0:1024], wq_area[:, 1024:2048]
        q1t = wq_area[:, :].rearrange("p (i d) -> p i d", i=NT)
        w_abs = sb("w_abs", [P, 2])
        w_tot = sb("w_tot", [P, 2])
        w_inv = sb("w_inv", [P, 2])
        w_up_scaled = sb("w_up_scaled", [P, 1])
        wt_area = sb("wt_area", [P, 2048])
        w_now = wt_area[:, :].rearrange("p (u t c) -> p u t c", u=2, t=2)
        w_t = wt_area[:, :].rearrange("p (n c) -> p n c", n=2)
        q2T = wt_area[:, 0:512].bitcast(BF16).rearrange("p (t a n) -> p t a n", t=2, a=KU)
        wc_area = sb("wc_area", [P, 1024])
        w_c = wc_area[:, :].bitcast(BF16).rearrange("p (n c) -> p n c", n=2)
        q2t = wc_area[:, :].rearrange("p (t c) -> p t c", t=2)
        tern = sb("tern", [P, 2, KD * UP], BF16)
        amax1, m1, qs1, f1, fsq, guard2, amax2, m2, qs2, f2 = (
            sb(n, [P, NT]) for n in "amax1 m1 qs1 f1 fsq guard2 amax2 m2 qs2 f2".split())

        def named(names):
            return [sem(name) for name in names.split()]

        cst_in, small_in, x_in, gate_in, wq_in, sw_in, w_in, xf_out, out_done = named(
            "cst_in small_in x_in gate_in wq_in sw_in w_in xf_out out_done")
        xg_in = named(" ".join(f"xg_in{u}" for u in range(UNROLL)))
        y_out = named(" ".join(f"y_out{u}" for u in range(UNROLL)))
        yg_in = [named(" ".join(f"yg_in{i}_{k}" for k in range(TOPK))) for i in range(NT)]
        filled, cond_ready, rows_psum, rows_ready, xT_psum, xT_ready, logits_psum, scores_ready = named(
            "filled cond_ready rows_psum rows_ready xT_psum xT_ready logits_psum scores_ready")
        w_abs_ready, w_tot_psum, w_inv_ready, w_t_ready, tern_ready = named(
            "w_abs_ready w_tot_psum w_inv_ready w_t_ready tern_ready")
        shared_gu_ready, shared_sg_ready, shared_h_ready, shared_y_done = named(
            "shared_gu_ready shared_sg_ready shared_h_ready shared_y_done")
        base_ready, chosen_ready, rank_psum, place_ready, tile_e_ready, tile_e_psum, expert_ready = named(
            "base_ready chosen_ready rank_psum place_ready tile_e_ready tile_e_psum expert_ready")
        tile8_ready, hot_ready, token_tile_ready, hot_used, slots_ready, now_ready, now_seen = named(
            "tile8_ready hot_ready token_tile_ready hot_used slots_ready now_ready now_seen")
        xa_psum, xgT_ready, gu_ready, sg_ready, h_ready, w_now_ready, y_psum, y_copied = named(
            "xa_psum xgT_ready gu_ready sg_ready h_ready w_now_ready y_psum y_copied")
        fetch_ready, xc_psum, xcT_ready, hd_psum = named("fetch_ready xc_psum xcT_ready hd_psum")
        qs1_ready, q1t_ready, q1_ready, q1T_psum, q1T_ready = named("qs1_ready q1t_ready q1_ready q1T_psum q1T_ready")
        up_psum, r_ready, r2_ready, mixed_ready, f_psum = named("up_psum r_ready r2_ready mixed_ready f_psum")
        qs2_ready, q2t_ready, q2_ready, q2T_psum, q2T_ready, d_psum, final_ready = named(
            "qs2_ready q2t_ready q2_ready q2T_psum q2T_ready d_psum final_ready")
        match_ready, weight_ready, diag_w_ready, sums_psum, x_ready = named(
            "match_ready weight_ready diag_w_ready sums_psum x_ready")
        dve_chain = sem("dve_chain")

        block = ctx.enter_context(nc.Block())
        SH = SHARED * NPAIR
        AHEAD = 3
        WCHUNK = 4
        W_FIRST = 2 * WCHUNK
        flat2 = "p t c -> p (t c)"

        @block.sync
        def _(sp):
            sp.dma_start(cst[:, :], consts).then_inc(cst_in, 16)
            sp.dma_start(subj[:, :], subj_rows).then_inc(small_in, 16)
            sp.dma_start(bias_s[:, :], bias).then_inc(small_in, 16)
            sp.dma_start(cond_w[:, :, :, :], cond).then_inc(small_in, 16)
            sp.dma_start(X[:, :, :], x).then_inc(x_in, 16)
            sp.dma_start(gate_s[:, :, :], gate).then_inc(gate_in, 16)
            sp.dma_start(W[:, E:EA, :], experts[E:EA].rearrange("e p c -> p e c")).then_inc(sw_in, 16)

            def load_experts(e):
                sp.dma_start(W[:, e:e + WCHUNK, :], experts[e:e + WCHUNK].rearrange("e p c -> p e c")).then_inc(w_in, 16)

            for e in range(0, W_FIRST, WCHUNK):
                load_experts(e)
            sp.wait_ge(rows_ready, NT)
            sp.dma_start(xf_dram.rearrange("(i p) d -> p i d", p=P), rows).then_inc(xf_out, 16)
            for e in range(W_FIRST, E, WCHUNK):
                load_experts(e)

            y_rows = y_dram.rearrange("(p s t) d -> p s (t d)", p=P, t=2)
            for u in range(UNROLL):
                sp.wait_ge(y_copied, u + 1)
                sp.dma_start(y_rows[:, u, :], yv[:, u, :]).then_inc(y_out[u], 16)
            sp.dma_start(up_s, w_up).then_inc(wq_in, 16)
            sp.dma_start(down_s, w_down).then_inc(wq_in, 16)
            with sp.Fori(1, ROUNDS) as it:
                for u in range(UNROLL):
                    sp.wait_ge(y_copied, it * UNROLL + (u + 1))
                    sp.dma_start(y_rows[:, bass.ds(it * UNROLL + u, 1), :].rearrange("p a c -> p (a c)"), yv[:, u, :]
                                 ).then_inc(y_out[u], 16)
            for i in range(NT):
                sp.wait_ge(final_ready, i + 1)
                sp.dma_start(out[i], X[:, i, :]).then_inc(out_done, 16)
            sp.wait_ge(out_done, 16 * NT)

        @block.gpsimd
        def _(pool):
            nc.gpsimd.memset(ones[:, :], 1.0)
            nc.gpsimd.memset(onesb[:, :], 1.0)
            nc.gpsimd.memset(magic[:, :], MAGIC)
            nc.gpsimd.memset(neg_magic[:, :], -MAGIC)
            nc.gpsimd.memset(gmax[:, :, GROUPS:], -1.0)
            pool.wait_ge(cst_in, 16)
            nc.gpsimd.tensor_copy(lowerb[:, :], lower)
            nc.gpsimd.tensor_copy(iota_k[:, :, :], iota.unsqueeze(2).broadcast_to([P, P, TOPK])).then_inc(filled, 1)

            def gather(s0, u):
                nc.gpsimd.tensor_copy(now[:, u, :], slot_token[:, bass.ds(s0 * 2 + 2 * u, 2)]).then_inc(now_ready, 1)
                pool.wait_ge(now_ready, s0 + (u + 1))
                pool.sem_inc(now_seen, 1)
                for t in range(2):
                    nc.gpsimd.indirect_dma_start(xg[:, u, t, :], None, xf_dram,
                                                 bass.IndirectOffsetOnAxis(now[:, u, t:t + 1], 0)).then_inc(xg_in[u], 16)

            pool.wait_ge(xf_out, 16)
            pool.wait_ge(slots_ready, 1)
            for u in range(UNROLL):
                gather(0, u)
            with pool.Fori(1, ROUNDS) as it:
                for u in range(UNROLL):
                    pool.wait_ge(xa_psum, it * UNROLL + (u + 1 - UNROLL))
                    gather(it * UNROLL, u)
            pool.wait_ge(fetch_ready, 1)
            for u in range(UNROLL):
                pool.wait_ge(y_out[u], 16 * ROUNDS)
            for i in range(NT):
                for k in range(TOPK):
                    nc.gpsimd.indirect_dma_start(yg[:, i, k, :], None, y_dram,
                                                 bass.IndirectOffsetOnAxis(fetch[:, i, k:k + 1], 0)).then_inc(yg_in[i][k], 16)

        def experts_of(engine, s0, steps):
            _, es = nc.values_load_multi_w_load_instructions(
                expert_of[0:1, bass.ds(s0 * 2, 2 * steps)], engines=[engine], min_val=0, max_val=E - 1,
                skip_runtime_bounds_check_because="the row counts experts that end and is capped at E - 1")
            return es

        def tiles_in(u, last):
            return LAST_TILES if last and u == UNROLL - 1 else 2

        def halfbank(b):
            return ps[:, b, :].rearrange("p (t c) -> p t c", t=2)

        @block.tensor
        def _(pe):
            T = nc.tensor
            pe.wait_ge(x_in, 16)
            for i in range(NT):
                pe.wait_ge(cond_ready, i // 2 + 1)
                T.matmul(halfbank(i // 2)[:, i % 2, :], cond_bd[:, 0, i, :], X[:, i, :], start=True, stop=True).then_inc(rows_psum, 1)
            pe.wait_ge(filled, 1)
            for q in range(NPAIR):
                pe.wait_ge(rows_ready, 2 * q + 2)
                if q >= 2:
                    pe.wait_ge(xT_ready, q - 1)
                for t in range(2):
                    for k in range(KD):
                        at = k * 256 + t * P
                        mm = T.transpose(ps[:, 4 + q % 2, at:at + P], rows[:, 2 * q + t, k * P:(k + 1) * P], ident)
                mm.then_inc(xT_psum, 1)
            pe.wait_ge(gate_in, 16)
            for i in range(NT):
                pe.wait_ge(xT_ready, i // 2 + 1)
                for k in range(KD):
                    mm = T.matmul(ps[:, 7, i * E:(i + 1) * E], xT[:, k, i * P:(i + 1) * P], gate_s[:, k, :],
                                  start=(k == 0), stop=(k == KD - 1))
            mm.then_inc(logits_psum, 1)

            def sh_gate_up(s):
                e, q = E + s // NPAIR, s % NPAIR
                for c in range(2):
                    for k in range(KD):
                        at = k * 256 + c * INTER
                        mm = T.matmul(halfbank(4 + s % 2)[:, c, :], W[:, e, at:at + INTER], xT[:, k, q * 256:(q + 1) * 256],
                                      start=(k == 0), stop=(k == KD - 1))
                mm.then_inc(shared_gu_ready, 1)

            def sh_down(s):
                e, q = E + s // NPAIR, s % NPAIR
                if e == E:
                    T.matmul(ps[:, q, :], ident, X[:, 2 * q:2 * q + 2, :].rearrange(flat2),
                             start=True, stop=False, skip_group_check=True)
                pe.wait_ge(shared_h_ready, s + 1)
                for t in range(2):
                    mm = T.matmul(halfbank(q)[:, t, :], h[:, s % 2, t, :], W[:, e, 512:512 + D],
                                  start=False, stop=(e == EA - 1), skip_group_check=True)
                mm.then_inc(shared_y_done, 1)

            def ranks():
                pe.wait_ge(chosen_ready, 1)
                T.matmul(ps[:, 7, 256:512], lowerb[:, :], chosen[:, :, :].rearrange("p i e -> p (i e)"), start=True, stop=False)
                for j in range(NT - 1):
                    mm = T.matmul(ps[:, 7, 256 + (j + 1) * E:512].rearrange("p (i e) -> p i e", e=E), onesb[:, :],
                                  chosen[:, j, :].unsqueeze(1).broadcast_to([P, NT - 1 - j, E]),
                                  start=False, stop=(j == NT - 2))
                for j in range(NT):
                    mm = T.matmul(ps[:, 7, 0:E], onesb[:, :], chosen[:, j, :], start=(j == 0), stop=(j == NT - 1))
                mm.then_inc(rank_psum, 1)

            def tile_experts():
                pe.wait_ge(tile_e_ready, 1)
                pe.wait_ge(place_ready, 1)
                T.matmul(ps[0:1, 7, 64:64 + TILES], tile_e[:, :], ident[:, 0:TILES], start=True, stop=True).then_inc(tile_e_psum, 1)

            def invert(i):
                pe.wait_ge(token_tile_ready, i + 1)
                pe.wait_ge(expert_ready, 1)
                for k in range(TOPK):
                    mm = T.matmul(ps[:, 7, 160:160 + TILES], hot_row[:, i % HOT, :, k], token_tile[:, i % HOT, :, k],
                                  start=(i == 0 and k == 0), stop=(i == NT - 1 and k == TOPK - 1))
                mm.then_inc(hot_used, 1)

            pe.wait_ge(sw_in, 16)
            sh_gate_up(0)
            sh_gate_up(1)
            sh_down(0)
            ranks()
            sh_gate_up(2)
            sh_down(1)
            tile_experts()
            sh_gate_up(3)
            sh_down(2)
            sh_gate_up(4)
            invert(0)
            invert(1)
            sh_down(3)
            invert(2)
            invert(3)
            sh_gate_up(5)
            for i in range(4, NT):
                invert(i)
            for s in range(4, SH):
                sh_down(s)
                if s + 2 < SH:
                    sh_gate_up(s + 2)

            def turn_in(s0, u, n=2):
                pe.wait_ge(xg_in[u % UNROLL], s0 * (32 // UNROLL) + 32 * (u // UNROLL + 1))
                for t in range(n):
                    for k in range(KD):
                        at = (2 * t + k) * P
                        mm = T.transpose(ps[:, u % 2, at:at + P], xg[:, u % UNROLL, t, k * P:(k + 1) * P], ident)
                mm.then_inc(xa_psum, 1)

            def gate_up(s0, u, n=2):
                pe.wait_ge(w_now_ready, s0 + (u + 1))
                pe.wait_ge(xgT_ready, s0 + (u + 1))
                for t in range(n):
                    for c in range(2):
                        for k in range(KD):
                            at = k * 256 + c * INTER
                            mm = T.matmul(halfbank(2 + u % 2)[:, t, c * P:(c + 1) * P], w_now[:, u % 2, t, at:at + INTER],
                                          xgT[:, u % 2, t, k, :], start=(k == 0), stop=(k == KD - 1))
                mm.then_inc(gu_ready, 1)

            def down(es, s0, u, n=2, first=False):
                pe.wait_ge(h_ready, s0 + (u + 1))
                if not first:
                    pe.wait_ge(y_copied, s0 + (u - 1))
                for t, e in enumerate(es[2 * u:2 * u + n]):
                    mm = T.matmul(halfbank(6 + u % 2)[:, t, :], h[:, u % 2, t, :],
                                  W[:, bass.ds(e, 1), 512:512 + D], start=True, stop=True)
                mm.then_inc(y_psum, 1)

            def round_(s0, first=False, last=False):
                es = experts_of(mybir.EngineType.PE, s0, UNROLL)
                for u in range(UNROLL):
                    if not last or u + 2 < UNROLL:
                        turn_in(s0, u + 2, tiles_in(u + 2, last))
                    if not last or u + 1 < UNROLL:
                        gate_up(s0, u + 1, tiles_in(u + 1, last))
                    down(es, s0, u, tiles_in(u, last), first and u < 2)

            pe.wait_ge(slots_ready, 1)
            pe.wait_ge(base_ready, 2)
            turn_in(0, 0)
            turn_in(0, 1)
            pe.wait_ge(w_in, 16 * (E // WCHUNK))
            pe.wait_ge(base_ready, NPAIR)
            gate_up(0, 0)
            round_(0, first=True)
            with pe.Fori(1, ROUNDS - 1) as it:
                round_(it * UNROLL)
            round_(STEPS - UNROLL, last=True)

            def sums(i):
                if i >= 1:
                    pe.wait_ge(x_ready, i)
                pe.wait_ge(diag_w_ready, i + 1)
                for k in range(TOPK):
                    pe.wait_ge(yg_in[i][k], 16)
                    mm = T.matmul(ps[:, 6, 0:D], diag_w[:, i, k, :], yg[:, i, k, :], start=(k == 0), stop=(k == TOPK - 1))
                mm.then_inc(sums_psum, 1)

            def condition1(i):
                pe.wait_ge(x_ready, i + 1)
                if i == 0:
                    pe.wait_ge(cond_ready, NPAIR + 1)
                else:
                    pe.wait_ge(xcT_ready, i)
                for a in range(KD):
                    mm = T.matmul(ps[:, 0, a * P:(a + 1) * P], X[:, i, a * P:(a + 1) * P], cond_bd[:, 1, i, :],
                                  start=True, stop=True)
                mm.then_inc(xc_psum, 1)

            def hadamard1(i):
                pe.wait_ge(xcT_ready, i + 1)
                if i >= 1:
                    pe.wait_ge(q1T_ready, i)
                for a in range(KD):
                    mm = T.matmul(ps[:, 1, 0:D], xcT[:, a, i * P:(i + 1) * P], had_rows[a], start=(a == 0), stop=(a == KD - 1))
                mm.then_inc(hd_psum, 1)

            def turn1(i):
                pe.wait_ge(q1_ready, i + 1)
                for k in range(KD):
                    mm = T.transpose(ps[:, 1, k * P:(k + 1) * P], q1t[:, i, k * P:(k + 1) * P], ident)
                mm.then_inc(q1T_psum, 1)

            def up(i):
                pe.wait_ge(q1T_ready, i + 1)
                if i == 0:
                    pe.wait_ge(tern_ready, 1)
                if i >= 2:
                    pe.wait_ge(r_ready, i - 1)
                for m in range(KU):
                    for k in range(KD):
                        mm = T.matmul(ps[:, 2 + i % 2, m * P:(m + 1) * P], tern[:, 0, k * UP + m * P:k * UP + (m + 1) * P],
                                      q1T[:, k, i * P:(i + 1) * P], start=(k == 0), stop=(k == KD - 1))
                mm.then_inc(up_psum, 1)

            def hadamard2(i):
                pe.wait_ge(mixed_ready, i + 1)
                if i >= 2:
                    pe.wait_ge(q2T_ready, i - 1)
                for a in range(KU):
                    mm = T.matmul(ps[:, 4 + i % 2, a * P:(a + 1) * P], r4[i % 2][:, a, :], had, start=True, stop=True)
                mm.then_inc(f_psum, 1)

            def turn2(i):
                pe.wait_ge(q2_ready, i + 1)
                for a in range(KU):
                    mm = T.transpose(ps[:, 4 + i % 2, a * P:(a + 1) * P], q2t[:, i % 2, a * P:(a + 1) * P], ident)
                mm.then_inc(q2T_psum, 1)

            def down2(i):
                pe.wait_ge(q2T_ready, i + 1)
                if i >= 1:
                    pe.wait_ge(final_ready, i)
                for a in range(KU):
                    mm = T.matmul(ps[:, 7, 0:D], q2T[:, i % 2, a, :], tern[:, 1, a * D:(a + 1) * D],
                                  start=(a == 0), stop=(a == KU - 1))
                mm.then_inc(d_psum, 1)

            pe.wait_ge(w_abs_ready, 1)
            T.matmul(ps[:, 5, 0:2], ones[:, :], w_abs[:, :], start=True, stop=True).then_inc(w_tot_psum, 1)
            pe.wait_ge(y_copied, STEPS)
            SECOND_PE = ((sums, 0), (down2, 4), (turn1, 1), (hadamard2, 2), (condition1, 0), (up, 1), (hadamard1, 0),
                         (turn2, 3))
            for j in range(NT + 4):
                for step, lag in SECOND_PE:
                    if 0 <= j - lag < NT:
                        step(j - lag)

        @block.scalar
        def _(act):
            A = nc.scalar
            for i in range(NT):
                act.wait_ge(rows_psum, i // 2 * 2 + 2)
                A.activation(rows[:, i, :], halfbank(i // 2)[:, i % 2, :], ACT.Identity, bias=bias_row[:, i:i + 1]
                             ).then_inc(rows_ready, 1)
            act.wait_ge(logits_psum, 1)
            A.activation(scores[:, :, :].rearrange("p i e -> p (i e)"), ps[:, 7, 0:NT * E], ACT.Sigmoid).then_inc(scores_ready, 1)

            def sh_silu(s):
                act.wait_ge(shared_gu_ready, s + 1)
                A.activation(sg[:, s % 2, :, :].rearrange(flat2), halfbank(4 + s % 2)[:, 0, :], ACT.Silu).then_inc(shared_sg_ready, 1)

            def base(q):
                act.wait_ge(shared_y_done, SH - NPAIR + q + 1)
                A.copy(X[:, 2 * q:2 * q + 2, :].rearrange(flat2), ps[:, q, :]).then_inc(base_ready, 1)

            def scale_tile(i):
                act.wait_ge(hot_ready, i + 1)
                if i >= HOT:
                    act.wait_ge(hot_used, i + 1 - HOT)
                A.activation(token_tile[:, i % HOT, :, :], hot_tile[:, i % HOT, :, :], ACT.Copy, scale=token[:, i:i + 1]
                             ).then_inc(token_tile_ready, 1)

            for s in range(4):
                sh_silu(s)
            scale_tile(0)
            scale_tile(1)
            sh_silu(4)
            for i in range(2, NT):
                scale_tile(i)
            sh_silu(5)
            sh_silu(6)
            base(0)
            sh_silu(7)
            base(1)
            base(2)

            def copy_w(es, s0, u, n=2):
                if not isinstance(s0, int) or s0 + u >= 2:
                    act.wait_ge(gu_ready, s0 + (u - 1))
                for t, e in enumerate(es[:n]):
                    ins = A.copy(w_now[:, u % 2, t, :], W[:, bass.ds(e, 1), 0:KD * 2 * INTER].rearrange("p a c -> p (a c)"))
                ins.then_inc(w_now_ready, 1)

            act.wait_ge(expert_ready, 1)
            es = experts_of(mybir.EngineType.Activation, 0, 2)
            act.wait_ge(w_in, 16 * (E // WCHUNK))
            copy_w(es, 0, 0)
            base(NPAIR - 1)

            def copy_in(s0, u, n=2):
                act.wait_ge(xa_psum, s0 + (u + 1))
                A.copy(xgT_area[:, u % 2 * 512:u % 2 * 512 + n * D], ps[:, u % 2, 0:n * D]).then_inc(xgT_ready, 1)

            def silu(s0, u, n=2):
                act.wait_ge(gu_ready, s0 + (u + 1))
                A.activation(sg[:, u % 2, 0:n, :], halfbank(2 + u % 2)[:, 0:n, 0:INTER], ACT.Silu).then_inc(sg_ready, 1)

            def round_(s0, last=False):
                es = experts_of(mybir.EngineType.Activation, s0 + 2, UNROLL - 2 if last else UNROLL)
                for u in range(UNROLL):
                    if not last or u + 2 < UNROLL:
                        copy_in(s0, u + 2, tiles_in(u + 2, last))
                        copy_w(es[2 * u:], s0, u + 2, tiles_in(u + 2, last))
                    if not last or u + 1 < UNROLL:
                        silu(s0, u + 1, tiles_in(u + 1, last))

            copy_in(0, 0)
            copy_w(es[2:], 0, 1)
            copy_in(0, 1)
            silu(0, 0)
            with act.Fori(0, ROUNDS - 1) as it:
                round_(it * UNROLL)
            round_(STEPS - UNROLL, last=True)

            def diagonals(i):
                for k in range(TOPK):
                    ins = A.activation(diag_w[:, i, k, :], ident, ACT.Identity, scale=weight[:, i, k:k + 1])
                ins.then_inc(diag_w_ready, 1)

            act.wait_ge(weight_ready, 1)
            act.wait_ge(y_psum, STEPS)
            diagonals(0)
            act.wait_ge(w_inv_ready, 1)
            for n, w in enumerate((up_s, down_s)):
                ins = A.activation(w_t[:, n, :], w, ACT.Identity, bias=magic[:, :], scale=w_inv[:, n:n + 1])
            ins.then_inc(w_t_ready, 1)
            for i in range(1, AHEAD):
                diagonals(i)

            def copy_xc(i):
                act.wait_ge(xc_psum, i + 1)
                A.copy(xcT[:, :, i * P:(i + 1) * P], ps[:, 0, 0:D].rearrange("p (a n) -> p a n", a=KD)).then_inc(xcT_ready, 1)

            def round1(i):
                act.wait_ge(qs1_ready, i + 1)
                A.activation(q1t[:, i, :], ps[:, 1, 0:D], ACT.Identity, bias=magic[:, :], scale=qs1[:, i:i + 1]
                             ).then_inc(q1t_ready, 1)

            def copy_q1(i):
                act.wait_ge(q1T_psum, i + 1)
                A.activation(q1T[:, :, i * P:(i + 1) * P], ps[:, 1, 0:D].rearrange("p (k n) -> p k n", k=KD), ACT.Identity,
                             bias=neg_magic[:, :]).then_inc(q1T_ready, 1)

            def squared_relu(i):
                act.wait_ge(up_psum, i + 1)
                if i >= 2:
                    act.wait_ge(mixed_ready, i - 1)
                A.activation(r[i % 2], ps[:, 2 + i % 2, :].rearrange("p (m n) -> p m n", m=KU), ACT.Relu).then_inc(r_ready, 1)
                act.wait_ge(r_ready, i + 1)
                A.activation(r2[i % 2], r[i % 2], ACT.Square).then_inc(r2_ready, 1)

            def round2(i):
                act.wait_ge(qs2_ready, i + 1)
                if i >= 2:
                    act.wait_ge(q2T_psum, i - 1)
                A.activation(q2t[:, i % 2, :], ps[:, 4 + i % 2, :], ACT.Identity, bias=magic[:, :], scale=qs2[:, i:i + 1]
                             ).then_inc(q2t_ready, 1)

            def copy_q2(i):
                act.wait_ge(q2T_psum, i + 1)
                if i >= 2:
                    act.wait_ge(d_psum, i - 1)
                A.activation(q2T[:, i % 2, :, :], ps[:, 4 + i % 2, :].rearrange("p (a n) -> p a n", a=KU), ACT.Identity,
                             bias=neg_magic[:, :]).then_inc(q2T_ready, 1)

            SECOND_ACT = ((copy_q2, 4), (round1, 1), (round2, 3), (copy_q1, 1), (copy_xc, 0), (squared_relu, 1),
                          (diagonals, -AHEAD))
            for j in range(NT + 4):
                for step, lag in SECOND_ACT:
                    if 0 <= j - lag < NT:
                        step(j - lag)

        @block.vector
        def _(v):
            chained = [0]

            def link(ins):
                chained[0] += 1
                ins.then_inc(dve_chain, 1)
                v.wait_ge(dve_chain, chained[0])

            V = nc.vector

            def bc(ap, dims, shape):
                for d in dims:
                    ap = ap.unsqueeze(d)
                return ap.broadcast_to(shape)

            v.wait_ge(cst_in, 16)
            v.wait_ge(small_in, 48)
            link(V.tensor_copy(subj_f[:, :], subj[:, :]))
            link(V.tensor_tensor(subj_mask[:, :, :], bc(subj_f[:, :], [2], [P, NT, SUBJ]), bc(iota[:, 0:SUBJ], [1], [P, NT, SUBJ]),
                                 ALU.is_equal))
            link(V.tensor_tensor(bias_t[:, :, :], bc(bias_s[:, :], [1], [P, NT, SUBJ]), subj_mask[:, :, :], ALU.mult))
            V.tensor_reduce(bias_row[:, :], bias_t[:, :, :], AX.X, ALU.add)

            def spread(area):
                return area[:, :].rearrange("p (i n s) -> p i n s", i=NT, n=SUBJ)

            def condition(layer, cond_t, i0, n):
                at = slice(i0, i0 + n)
                link(V.tensor_tensor(cond_t[:, at, :, :], bc(cond_w[:, layer, :, :], [1], [P, n, SUBJ, S]),
                                     bc(subj_mask[:, at, :], [3], [P, n, SUBJ, S]), ALU.mult))
                link(V.tensor_reduce(cond_sel[:, layer, at, :], cond_t[:, at, :, :].rearrange("p i n s -> p i s n"), AX.X, ALU.add))
                V.tensor_tensor(cond_bd[:, layer, at, :].rearrange("p i (j s) -> p i j s", j=BPT),
                                bc(cond_sel[:, layer, at, :], [2], [P, n, BPT, S]),
                                bc(bc(diag, [1], [P, n, BPT]), [3], [P, n, BPT, S]), ALU.mult).then_inc(cond_ready, 1)

            for i in range(0, NT, 2):
                condition(0, spread(y_area), i, 2)
            for q in range(NPAIR):
                v.wait_ge(xT_psum, q + 1)
                V.tensor_copy(xT[:, :, q * 256:(q + 1) * 256], ps[:, 4 + q % 2, :].rearrange("p (k n) -> p k n", k=KD)
                              ).then_inc(xT_ready, 1)

            def sh_mul(s):
                v.wait_ge(shared_sg_ready, s + 1)
                V.tensor_tensor(h[:, s % 2, :, :].rearrange(flat2), sg[:, s % 2, :, :].rearrange(flat2),
                                halfbank(4 + s % 2)[:, 1, :], ALU.mult).then_inc(shared_h_ready, 1)

            groups = [P, NT, GROUPS, E // GROUPS]

            def grouped(t):
                return t[:, :, :].rearrange("p i (g m) -> p i g m", g=GROUPS)

            v.wait_ge(scores_ready, 1)
            link(V.tensor_reduce(gmax[:, :, 0:GROUPS], grouped(scores), AX.X, ALU.max))
            for i in range(NT):
                ins = V.max(gtop[:, i, :], gmax[:, i, 0:GROUPS])
            link(ins)
            link(V.memset(gtop[:, :, TOPK_G:], -1.0))
            for i in range(NT):
                ins = V.match_replace(grep[:, i, :], gtop[:, i, :], gmax[:, i, :], -2.0)
            link(ins)
            link(V.tensor_scalar(gmask[:, :, :], grep[:, :, 0:GROUPS], 0.0, None, ALU.is_lt))
            link(V.tensor_tensor(grouped(smask), grouped(scores), bc(gmask[:, :, :], [3], groups), ALU.mult))
            link(V.tensor_scalar(gmask[:, :, :], gmask[:, :, :], 1.0, None, ALU.subtract))
            sh_mul(0)
            link(V.tensor_tensor(grouped(smask), grouped(smask), bc(gmask[:, :, :], [3], groups), ALU.add))
            for i in range(NT):
                ins = V.max(stop8[:, i, :], smask[:, i, :])
            link(ins)
            link(V.memset(stop8[:, :, TOPK:], -1.0))
            for i in range(NT):
                ins = V.match_replace(srep[:, i, :], stop8[:, i, :], smask[:, i, :], -2.0)
            link(ins)
            link(V.tensor_scalar(smask[:, :, :], smask[:, :, :], 0.0, None, ALU.is_ge))
            V.scalar_tensor_tensor(chosen[:, :, :], srep[:, :, :], 0.0, smask[:, :, :], ALU.is_lt, ALU.mult).then_inc(chosen_ready, 1)
            v.wait_ge(chosen_ready, 1)
            sh_mul(1)
            v.wait_ge(rank_psum, 1)
            link(V.tensor_scalar(tiles_of[:, :], ps[:, 7, 0:E], 1.0 / P, 0.5 - 0.5 / P, ALU.mult, ALU.add))
            link(V.tensor_scalar(tiles_of[:, :], tiles_of[:, :], MAGIC, MAGIC, ALU.add, ALU.subtract))
            link(V.tensor_tensor_scan(tiles_end[:, :], ones[:, 0:E], tiles_of[:, :], 0.0, ALU.mult, ALU.add))
            link(V.tensor_tensor(tiles_from[:, :], tiles_end[:, :], tiles_of[:, :], ALU.subtract))
            link(V.tensor_scalar(begun[:, :], tiles_end[:, :], token[:, 0:1], None, ALU.is_le))
            V.tensor_reduce(tile_e[:, :], begun[:, :], AX.X, ALU.add).then_inc(tile_e_ready, 1)
            rank = ps[:, 7, 256:512].rearrange("p (i e) -> p i e", e=E)
            link(V.tensor_scalar(turnover[:, :, :], rank, 1.0 / P, 0.5 / P - 0.5, ALU.mult, ALU.add))
            link(V.tensor_scalar(turnover[:, :, :], turnover[:, :, :], MAGIC, MAGIC, ALU.add, ALU.subtract))
            link(V.scalar_tensor_tensor(turnover[:, :, :], turnover[:, :, :], 1.0 - P * TILES,
                                        bc(tiles_from[:, :], [1], [P, NT, E]), ALU.mult, ALU.add))
            V.scalar_tensor_tensor(place[:, :, :], rank, float(TILES), turnover[:, :, :], ALU.mult, ALU.add).then_inc(place_ready, 1)
            v.wait_ge(place_ready, 1)
            link(V.scalar_tensor_tensor(place[:, :, :], place[:, :, :], 1.0, chosen[:, :, :], ALU.add, ALU.mult))
            sh_mul(2)
            for i in range(NT):
                ins = V.max(place8[:, i, :], place[:, i, :])
            link(ins)
            link(V.tensor_scalar(turn8[:, :, :], place8[:, :, :], 1.0 / TILES, -0.5 - 0.5 / TILES, ALU.mult, ALU.add))
            link(V.tensor_scalar(part8[:, :, :], turn8[:, :, :], MAGIC, MAGIC, ALU.add, ALU.subtract))
            link(V.scalar_tensor_tensor(turn8[:, :, :], part8[:, :, :], -float(TILES), place8[:, :, :], ALU.mult, ALU.add))
            V.tensor_scalar(tile8[:, :, :], turn8[:, :, :], 1.0, None, ALU.subtract).then_inc(tile8_ready, 1)
            v.wait_ge(tile8_ready, 1)
            v.wait_ge(tile_e_psum, 1)
            V.tensor_scalar(expert_of[:, :], ps[0:1, 7, 64:64 + TILES], float(E - 1), None, ALU.min).then_inc(expert_ready, 1)

            def one_hot(i):
                if i >= HOT:
                    v.wait_ge(hot_used, i + 1 - HOT)
                V.tensor_tensor(hot_row[:, i % HOT, :, :], iota_k[:, :, :], bc(part8[:, i, 0:TOPK], [1], [P, P, TOPK]), ALU.is_equal)
                V.tensor_tensor(hot_tile[:, i % HOT, :, :], iota_k[:, 0:TILES, :], bc(tile8[:, i, 0:TOPK], [1], [P, TILES, TOPK]),
                                ALU.is_equal).then_inc(hot_ready, 1)

            for i in range(NT):
                one_hot(i)
                if i in (1, 4):
                    sh_mul(3 + i // 4)
            v.wait_ge(hot_used, NT)
            V.tensor_copy(slot_token[:, :], ps[:, 7, 160:160 + TILES]).then_inc(slots_ready, 1)
            sh_mul(5)
            sh_mul(6)
            sh_mul(7)
            link(V.tensor_tensor(scores[:, :, :], scores[:, :, :], chosen[:, :, :], ALU.mult))
            link(V.tensor_reduce(wsum[:, :], scores[:, :, :], AX.X, ALU.add))
            link(V.reciprocal(wrec[:, :], wsum[:, :]))
            link(V.scalar_tensor_tensor(scores[:, :, :], scores[:, :, :], ROUTE_SCALE, bc(wrec[:, :], [2], [P, NT, E]),
                                        ALU.mult, ALU.mult))
            V.tensor_scalar(fetch[:, :, :], place8[:, :, :], 1.0, None, ALU.subtract).then_inc(fetch_ready, 1)

            def match_places():
                v.wait_ge(xf_out, 16)
                each = [P, NT, TOPK, E]
                V.tensor_tensor(match, bc(place8[:, :, 0:TOPK], [3], each), bc(place[:, :, :], [2], each), ALU.is_equal
                                ).then_inc(match_ready, 1)

            def weigh_places():
                v.wait_ge(match_ready, 1)
                V.tensor_tensor(match, match, bc(scores[:, :, :], [2], [P, NT, TOPK, E]), ALU.mult).then_inc(match_ready, 1)

            def place_weights():
                v.wait_ge(match_ready, 2)
                V.tensor_reduce(weight[:, :, :], match, AX.X, ALU.add).then_inc(weight_ready, 1)

            def weight_sums():
                v.wait_ge(wq_in, 32)
                V.tensor_reduce(w_abs[:, 0:1], up_s, AX.X, ALU.add, apply_absolute_value=True)
                V.tensor_reduce(w_abs[:, 1:2], down_s, AX.X, ALU.add, apply_absolute_value=True).then_inc(w_abs_ready, 1)

            extras = [match_places, weigh_places, place_weights]

            def mul(s0, u, n=2):
                v.wait_ge(sg_ready, s0 + (u + 1))
                V.tensor_tensor(h[:, u % 2, 0:n, :], sg[:, u % 2, 0:n, :], halfbank(2 + u % 2)[:, 0:n, INTER:], ALU.mult
                                ).then_inc(h_ready, 1)

            def copy_y(s0, u, n=2, first=False):
                v.wait_ge(y_psum, s0 + (u + 1))
                if not first:
                    v.wait_ge(y_out[u], s0 * (16 // UNROLL))
                V.tensor_copy(yv[:, u, 0:n * D], ps[:, 6 + u % 2, 0:n * D]).then_inc(y_copied, 1)

            def round_(s0, first=False, last=False):
                for u in range(UNROLL):
                    if not last or u + 1 < UNROLL:
                        mul(s0, u + 1, tiles_in(u + 1, last))
                    copy_y(s0, u, tiles_in(u, last), first)
                    if first and u < len(extras):
                        extras[u]()

            mul(0, 0)
            round_(0, first=True)
            with v.Fori(1, ROUNDS - 1) as it:
                round_(it * UNROLL)
            round_(STEPS - UNROLL, last=True)
            weight_sums()
            v.wait_ge(w_tot_psum, 1)
            link(V.tensor_scalar(w_tot[:, :], ps[:, 5, 0:2], 1.0 / (UP * D), EPS, ALU.mult, ALU.max))
            V.reciprocal(w_inv[:, :], w_tot[:, :]).then_inc(w_inv_ready, 1)
            V.tensor_scalar(w_up_scaled[:, :], w_tot[:, 0:1], float(D) ** -0.5, None, ALU.mult)
            condition(1, spread(rows_area), 0, NT)
            v.wait_ge(w_t_ready, 1)
            link(V.tensor_scalar(w_c, w_t, MAGIC, 1.0, ALU.subtract, ALU.min))
            V.tensor_scalar(tern[:, :, :], w_c, -1.0, None, ALU.max).then_inc(tern_ready, 1)

            def add(i):
                v.wait_ge(sums_psum, i + 1)
                V.tensor_tensor(X[:, i, :], ps[:, 6, 0:D], X[:, i, :], ALU.add).then_inc(x_ready, 1)

            def stats1(i):
                v.wait_ge(hd_psum, i + 1)
                at = slice(i, i + 1)
                link(V.tensor_reduce(amax1[:, at], ps[:, 1, 0:D], AX.X, ALU.max, apply_absolute_value=True))
                link(V.tensor_scalar(m1[:, at], amax1[:, at], EPS * float(D) ** 0.5, 1.0 / QMAX, ALU.max, ALU.mult))
                V.reciprocal(qs1[:, at], m1[:, at]).then_inc(qs1_ready, 1)

            def clip1(i):
                v.wait_ge(q1t_ready, i + 1)
                V.tensor_scalar(q1t[:, i, :], q1t[:, i, :], MAGIC + QMAX, MAGIC - QMAX, ALU.min, ALU.max).then_inc(q1_ready, 1)

            def factors1(i):
                at = slice(i, i + 1)
                link(V.tensor_scalar(f1[:, at], m1[:, at], w_up_scaled[:, :], None, ALU.mult))
                link(V.scalar_tensor_tensor(fsq[:, at], f1[:, at], float(UP) ** -0.5, f1[:, at], ALU.mult, ALU.mult))
                link(V.reciprocal(guard2[:, at], fsq[:, at]))
                V.tensor_scalar(guard2[:, at], guard2[:, at], EPS / QMAX, None, ALU.mult)

            def mix(i):
                a, b, c = (t[i % 2].rearrange("p (c d) n -> p c d n", c=2) for t in (r2, r3, r4))
                v.wait_ge(r2_ready, i + 1)
                V.tensor_tensor(b[:, :, 0, :], a[:, :, 0, :], a[:, :, 1, :], ALU.add)
                link(V.tensor_tensor(b[:, :, 1, :], a[:, :, 0, :], a[:, :, 1, :], ALU.subtract))
                if i >= 2:
                    v.wait_ge(f_psum, i - 1)
                V.tensor_tensor(c[:, 0, :, :], b[:, 0, :, :], b[:, 1, :, :], ALU.add)
                V.tensor_tensor(c[:, 1, :, :], b[:, 0, :, :], b[:, 1, :, :], ALU.subtract).then_inc(mixed_ready, 1)

            def stats2(i):
                v.wait_ge(f_psum, i + 1)
                at = slice(i, i + 1)
                link(V.tensor_reduce(amax2[:, at], ps[:, 4 + i % 2, :], AX.X, ALU.max, apply_absolute_value=True))
                link(V.scalar_tensor_tensor(m2[:, at], amax2[:, at], 1.0 / QMAX, guard2[:, at], ALU.mult, ALU.max))
                V.reciprocal(qs2[:, at], m2[:, at]).then_inc(qs2_ready, 1)
                V.scalar_tensor_tensor(f2[:, at], m2[:, at], w_tot[:, 1:2], fsq[:, at], ALU.mult, ALU.mult)

            def clip2(i):
                v.wait_ge(q2t_ready, i + 1)
                q = q2t[:, i % 2, :]
                V.tensor_scalar(q, q, MAGIC + QMAX, MAGIC - QMAX, ALU.min, ALU.max).then_inc(q2_ready, 1)

            def final(i):
                v.wait_ge(d_psum, i + 1)
                V.scalar_tensor_tensor(X[:, i, :], ps[:, 7, 0:D], f2[:, i:i + 1], X[:, i, :], ALU.mult, ALU.add
                                       ).then_inc(final_ready, 1)

            SECOND_DVE = ((stats1, 1), (mix, 2), (clip1, 1), (add, 0), (clip2, 3), (factors1, 1), (stats2, 2), (final, 4))
            for j in range(NT + 4):
                for step, lag in SECOND_DVE:
                    if 0 <= j - lag < NT:
                        step(j - lag)


def hadamard(n):
    m = np.ones((1, 1), np.float32)
    while m.shape[0] < n:
        m = np.block([[m, m], [m, -m]])
    return m


def constants():
    c = np.zeros((P, C_END), np.float32)
    c[:, C_ID:C_ID + P] = np.eye(P)
    c[:, C_HAD:C_HAD + 3 * P] = np.concatenate([hadamard(P), hadamard(P), -hadamard(P)], 1)
    c[:, C_LOWER:C_LOWER + P] = np.arange(P)[:, None] < np.arange(P)
    c[:, C_IOTA:C_IOTA + P] = np.arange(P)
    c[:, C_DIAG:C_DIAG + BPT] = np.arange(P)[:, None] // S == np.arange(BPT)
    c[:, C_TOKEN:C_TOKEN + NT] = np.arange(P)[:, None] + P * np.arange(NT)
    return c


def kernel(**inputs):
    import concourse.bacc as _bacc
    from concourse.bass_utils import run_bass_kernel_spmd as _run

    a = {k: np.asarray(v) for k, v in inputs.items()}
    subj = a["itok_B_0_7"]
    x = a["x"].reshape(NT, P, D).transpose(1, 0, 2)

    def cond(w):
        return np.tile(w.transpose(1, 0, 2), (BPT, 1, 1))

    def inward(w):
        t = np.swapaxes(w, -1, -2)
        t = t.reshape(*t.shape[:-2], KD, P, t.shape[-1])
        return np.swapaxes(t, -3, -2)

    def expert(w1, w3, w2):
        gu = np.concatenate([inward(w1), inward(w3)], -1).reshape(-1, P, KD * 2 * INTER)
        return np.concatenate([gu, np.swapaxes(w2, -1, -2)], -1)

    sw = [a["L0_ffn_sw1"].reshape(SHARED, INTER, D), a["L0_ffn_sw3"].reshape(SHARED, INTER, D),
          a["L0_ffn_sw2"].reshape(D, SHARED, INTER).transpose(1, 0, 2)]
    arrays = {
        "x": x,
        "subj_rows": np.repeat(subj.reshape(NT, BPT).T, S, axis=0),
        "bias": np.tile(a["fside_8xS_0"].T, (BPT, 1)),
        "gate": inward(a["L0_ffn_gate_w"]),
        "experts": np.concatenate([expert(a["L0_ffn_w11"], a["L0_ffn_w33"], a["L0_ffn_w22"]), expert(*sw)]),
        "cond": np.stack([cond(a["L0_cond_weights"]), cond(a["L1_cond_weights"])], 1),
        "w_up": inward(a["L1_ffn_w_up"]).reshape(P, KD * UP),
        "w_down": a["L1_ffn_w_down"].T.reshape(KU, P, D).transpose(1, 0, 2).reshape(P, KU * D),
        "consts": constants(),
    }
    arrays = {k: np.ascontiguousarray(v) for k, v in arrays.items()}
    nc = _bacc.Bacc("TRN2", target_bir_lowering=False, num_devices=1)
    aps = {k: nc.dram_tensor(f"in_{k}", v.shape, mybir.dt.from_np(v.dtype), kind="ExternalInput").ap() for k, v in arrays.items()}
    out = nc.dram_tensor("out_0", (NT, P, D), F32, kind="ExternalOutput").ap()
    xf_dram = nc.dram_tensor("xf_rows", (N, D), F32).ap()
    y_dram = nc.dram_tensor("y_rows", (P * TILES, D), F32).ap()
    build(nc, out=out, xf_dram=xf_dram, y_dram=y_dram, **aps)
    res = _run(nc, [{f"in_{k}": v for k, v in arrays.items()}], core_ids=[0])
    return res.results[0]["out_0"].reshape(B, S, D)
```
